# Optimizing a Trainium2 kernel written in Bass

```python
import numpy as np
import jax
import jax.numpy as jnp

def _softmax(x, axis=-1):
    return jax.nn.softmax(x, axis=axis)

def _gelu(x):
    return jax.nn.gelu(x, approximate=True)

def _silu(x):
    return jax.nn.silu(x)

def _sigmoid(x):
    return jax.nn.sigmoid(x)

def _layernorm(x, axis=-1, eps=1e-05):
    m = jnp.mean(x, axis=axis, keepdims=True)
    v = jnp.var(x, axis=axis, keepdims=True)
    return (x - m) / jnp.sqrt(v + eps)

def _scatter_add(tgt, idx, src, axis=0):
    return tgt.at[idx].add(src)

def _segment_sum(src, seg, n):
    return jax.ops.segment_sum(src, seg, n)
kernel_name = 'mk_adj_resnorm_d2_adj_r2_654072'

def setup_inputs(seed: int=0):
    np.random.seed(seed)
    _w = jnp.asarray

    def _rec_inputs():
        import jax
        import jax.numpy as jnp
        _gk = jax.random.key(seed)
        x = -0.003407 + 1.001 * jax.random.normal(jax.random.fold_in(_gk, 1), (64, 128, 64), jnp.float32)
        _w = (1.0 + jnp.arange(128, dtype=jnp.float32)) ** (-0.5)
        _w = _w / _w.mean()
        _pij = jnp.clip(0.03125 * _w[:, None] * _w[None, :], 0.0, 1.0)
        _a = jax.random.uniform(jax.random.fold_in(_gk, 2), (64, 128, 128)) < _pij
        _a = jnp.logical_or(_a, jnp.swapaxes(_a, -1, -2))
        _a = jnp.logical_or(_a, jnp.eye(128, dtype=bool))
        _af = _a.astype(jnp.float32)
        _af = _af * jax.random.uniform(jax.random.fold_in(_gk, 3), (64, 128, 128), jnp.float32, 0.05, 0.999927)
        adj = _af
        return (x, adj)
    x, adj = _rec_inputs()

    def _L0_gnn_setup():
        import jax, jax.numpy as jnp
        import numpy as np
        N_RBF = 150
        GAMMA = 10.0
        LOG2 = float(np.log(2.0))

        def ssp(v):
            return jax.nn.softplus(v) - LOG2
        key = jax.random.key(seed)
        k1, k2, k3, k4 = jax.random.split(key, 4)
        B, N, F = (16, 128, 64)
        x = jax.random.normal(k1, (B, N, F), dtype=jnp.float32)
        distances = jax.random.uniform(k2, (B, N, N), dtype=jnp.float32)
        W1 = jax.random.normal(k3, (N_RBF, 64), dtype=jnp.float32) / np.sqrt(N_RBF)
        b1 = jnp.zeros((64,), dtype=jnp.float32)
        W2 = jax.random.normal(k4, (64, 64), dtype=jnp.float32) / np.sqrt(64)
        b2 = jnp.zeros((64,), dtype=jnp.float32)
        return {'x': x, 'distances': distances, 'W1': W1, 'b1': b1, 'W2': W2, 'b2': b2}
    _L0_gnn_all = _L0_gnn_setup()
    _L0_gnn_in = {k: v for k, v in _L0_gnn_all.items() if k in ('W1', 'b1', 'W2', 'b2')}
    del _L0_gnn_all

    def _L1_gnn_setup():
        import jax, jax.numpy as jnp
        import numpy as np
        B, N, IN_C, OUT_C, K_ORDERS = (16, 512, 64, 64, 4)

        def _get_laplacian(graph):
            deg = jnp.sum(graph, axis=-1)
            d = deg ** (-0.5)
            d = jnp.where(jnp.isnan(d), 0.0, d)
            eye = jnp.eye(graph.shape[1], dtype=graph.dtype)
            L = eye[None] - d[:, :, None] * graph * d[:, None, :]
            L = jnp.where(jnp.isnan(L), 0.0, L)
            L = jnp.where(jnp.isinf(L), 0.0, L)
            return L

        def _cheb_polynomials(L, k_orders):
            b, n = (L.shape[0], L.shape[1])
            T0 = jnp.broadcast_to(jnp.eye(n, dtype=L.dtype)[None], (b, n, n))
            Ts = [T0]
            if k_orders > 1:
                Ts.append(L)
                for _ in range(2, k_orders):
                    Ts.append(2.0 * jnp.matmul(L, Ts[-1]) - Ts[-2])
            return jnp.stack(Ts, axis=0)
        key = jax.random.key(seed)
        k1, k2, k3, k4 = jax.random.split(key, 4)
        inputs = jax.random.normal(k1, (B, N, IN_C), dtype=jnp.float32)
        graph = jax.random.uniform(k2, (B, N, N), dtype=jnp.float32)
        std = float(np.sqrt(2.0 / (IN_C + OUT_C)))
        weight = jax.random.normal(k3, (K_ORDERS, 1, IN_C, OUT_C), dtype=jnp.float32) * std
        bias = jax.random.normal(k4, (1, 1, OUT_C), dtype=jnp.float32) * 0.01
        return {'inputs': inputs, 'graph': graph, 'weight': weight, 'bias': bias}
    _L1_gnn_all = _L1_gnn_setup()
    _L1_gnn_in = {k: v for k, v in _L1_gnn_all.items() if k in ('weight', 'bias')}
    del _L1_gnn_all
    return {'x': x, 'adj': adj, 'L0_gnn_W1': _L0_gnn_in['W1'], 'L0_gnn_b1': _L0_gnn_in['b1'], 'L0_gnn_W2': _L0_gnn_in['W2'], 'L0_gnn_b2': _L0_gnn_in['b2'], 'L1_gnn_weight': _L1_gnn_in['weight'], 'L1_gnn_bias': _L1_gnn_in['bias']}

def reference(x, adj, L0_gnn_W1, L0_gnn_b1, L0_gnn_W2, L0_gnn_b2, L1_gnn_weight, L1_gnn_bias):
    import jax
    import jax.numpy as jnp

    def _L0_gnn_ref(x, distances, W1, b1, W2, b2):
        import jax, jax.numpy as jnp
        import numpy as np
        N_RBF = 150
        GAMMA = 10.0
        LOG2 = float(np.log(2.0))

        def ssp(v):
            return jax.nn.softplus(v) - LOG2
        centers = 0.1 * jnp.arange(N_RBF, dtype=distances.dtype)
        e_k = jnp.exp(-GAMMA * (distances[..., None] - centers) ** 2)
        h = ssp(jnp.einsum('bijk,kf->bijf', e_k, W1) + b1)
        w_l = ssp(jnp.einsum('bijf,fg->bijg', h, W2) + b2)
        return jnp.sum(x[:, :, None, :] * w_l, axis=2)

    def _L1_gnn_ref(inputs, graph, weight, bias):
        import jax, jax.numpy as jnp
        import numpy as np
        B, N, IN_C, OUT_C, K_ORDERS = (16, 512, 64, 64, 4)

        def _get_laplacian(graph):
            deg = jnp.sum(graph, axis=-1)
            d = deg ** (-0.5)
            d = jnp.where(jnp.isnan(d), 0.0, d)
            eye = jnp.eye(graph.shape[1], dtype=graph.dtype)
            L = eye[None] - d[:, :, None] * graph * d[:, None, :]
            L = jnp.where(jnp.isnan(L), 0.0, L)
            L = jnp.where(jnp.isinf(L), 0.0, L)
            return L

        def _cheb_polynomials(L, k_orders):
            b, n = (L.shape[0], L.shape[1])
            T0 = jnp.broadcast_to(jnp.eye(n, dtype=L.dtype)[None], (b, n, n))
            Ts = [T0]
            if k_orders > 1:
                Ts.append(L)
                for _ in range(2, k_orders):
                    Ts.append(2.0 * jnp.matmul(L, Ts[-1]) - Ts[-2])
            return jnp.stack(Ts, axis=0)
        L = _get_laplacian(graph)
        mul_l = _cheb_polynomials(L, K_ORDERS)
        res = jnp.einsum('kbnm,bmc->kbnc', mul_l, inputs)
        out = jnp.einsum('kbnc,kco->bno', res, weight[:, 0])
        return out + bias
    x = _layernorm(x + _L0_gnn_ref(x, adj, L0_gnn_W1, L0_gnn_b1, L0_gnn_W2, L0_gnn_b2), axis=-1)
    x = _layernorm(x + _L1_gnn_ref(x, adj, L1_gnn_weight, L1_gnn_bias), axis=-1)
    return x

_drawn_inputs = setup_inputs


def setup_inputs(seed=0):
    import zlib

    import numpy as np

    out = dict(_drawn_inputs(seed))
    spreads = {'L0_gnn_b1': (0.0, 0.1), 'L0_gnn_b2': (0.0, 0.1)}
    factors = {'L1_gnn_bias': 8.0}
    for name, (base, spread) in spreads.items():
        noise = np.random.default_rng([zlib.crc32(name.encode()), seed]).standard_normal(out[name].shape)
        drawn = base * np.exp(spread * noise) if base else spread * noise
        out[name] = jnp.asarray(drawn.astype(out[name].dtype))
    for name, factor in factors.items():
        out[name] = (out[name] * factor).astype(out[name].dtype)
    return out
```

```python
import numpy as np
import concourse.bass as bass
from concourse import mybir
from contextlib import ExitStack

B, N, F = 64, 128, 64
NRBF = 150
LOG2 = float(np.log(2.0))
EPS = 1e-5

TILES = N // 2
OCT = 8
OCTETS = TILES // OCT
CAPS = [62, 40, 34, 30, 28, 28, 26, 26, 26, 26, 24, 24, 22, 20, 20, 20,
        20, 20, 20, 18, 18, 18, 18, 18, 20, 18, 18, 18, 18, 18, 16, 16,
        18, 18, 18, 16, 16, 16, 16, 16, 16, 16, 16, 16, 16, 16, 16, 16,
        16, 16, 16, 16, 16, 16, 16, 16, 16, 16, 16, 16, 16, 16, 16, 16]
SLOTMAX = -(-max(CAPS) // 8) * 8

ORDER = list(range(OCTETS - 1, -1, -1))
LEVELS = []
ITEMS = 0
for o in ORDER:
    caps = CAPS[OCT * o:OCT * o + OCT]
    for lev in range(caps[0] // 2):
        live = sum(c > 2 * lev for c in caps)
        LEVELS.append((o, lev, live, ITEMS))
        ITEMS += live
UB = 8
BI = UB * OCT
NBLK = -(-ITEMS // BI)
UNITS = NBLK * UB
UC = OCT * 128
SORT_AHEAD = 16

PARTS = 6
PROWS = UB * 2 * PARTS
ONES = 96
KROWS = ONES + 3
KCH = 3
DMAX = 3.0
ZMAX = 40.0
PMAX = 2.0 ** 60
GBLK = N // (2 * UB)
GSTEPS = UB
LTB = 16
GR = 8


def runs_of_unit(q):
    out = []
    for o, lev, live, at in LEVELS:
        a, b = max(at, OCT * q), min(at + live, OCT * q + OCT)
        if a < b:
            out.append((a - OCT * q, b - a, OCT * o + a - at, lev == 0, o))
    return out


def build(nc, x, adj, W1, b1, W2, b2, WL, biasL, c_e, c_f, out):
    f32, bf16, i32 = mybir.dt.float32, mybir.dt.bfloat16, mybir.dt.int32
    ALU = mybir.AluOpType
    ACT = mybir.ActivationFunctionType
    AX = mybir.AxisListType
    ctx = ExitStack()
    with ctx:
        def sb(name, shape, dt=f32):
            return ctx.enter_context(nc.sbuf_tensor(name, shape, dt))

        def pb(name, shape, dt=f32):
            return ctx.enter_context(nc.psum_tensor(name, shape, dt))

        def sem(name):
            return ctx.enter_context(nc.semaphore(name))

        V = sb("V", [128, TILES, N])
        LT = sb("LT", [128, B, N])
        PR = sb("PR", [128, TILES, 128])
        X = sb("X", [128, B, F])
        SRT = sb("SRT", [128, TILES, SLOTMAX])
        D = sb("D", [128, NBLK * BI, 2])
        BUF = sb("BUF", [128, 2, OCT, UB * 2 * PARTS], bf16)
        PT = sb("PT", [128, 2, UC], bf16)
        r1 = sb("r1", [128, BI, 2])
        dd = sb("dd", [128, BI, 2])
        dl = sb("dl", [128, BI, 2])
        e = sb("e", [128, 2, UC])
        t = sb("t", [128, UC])
        h = sb("h", [128, 2, UC])
        y = sb("y", [128, 2, UC])
        junk = sb("junk", [128, UC])
        ce = sb("ce", [128, KCH * UB * 128], mybir.dt.uint16)
        cf = sb("cf", [128, 1 + 128 + 64 + 128])
        identb = sb("identb", [128, 128], bf16)
        ident2 = sb("ident2", [128, 128])
        w1bd = sb("w1bd", [128, KCH, 128])
        w2bd = sb("w2bd", [128, 128])
        w1abs = sb("w1abs", [128, 128])
        b1c = sb("b1c", [128, 1])
        b2c = sb("b2c", [128, 1])
        b2p = sb("b2p", [128, 1])
        wl = sb("wl", [128, 4, 2 * F])
        biasr = sb("biasr", [128, F])
        cols = sb("cols", [128, 8])
        diag = sb("diag", [64, 64])
        C1 = sb("C1", [128, F])
        deg = sb("deg", [128, B])
        dinv = sb("dinv", [128, B])
        dinv2 = sb("dinv2", [128, B])
        enz = sb("enz", [128, B])
        mhalf = sb("mhalf", [128, B])
        stage = sb("stage", [128, 2, 4, 128])
        ie = sb("ie", [128, 4, 128])
        zc = sb("zc", [128, 8])
        okc = sb("okc", [128, OCTETS])
        okz = sb("okz", [128, 10])
        flagc = sb("flagc", [128, 8])
        flag = sb("flag", [1, 1], i32)
        onec = sb("onec", [128, 1])
        nl2 = sb("nl2", [128, 1])

        x1s = h[:, 0, :].rearrange("p (k b c) -> p k b c", k=2, b=GR)
        x1t = h[:, 1, :].rearrange("p (k b i) -> p k b i", k=2, b=GR // 2)
        b3s = e[:, 0, :].rearrange("p (k b c) -> p k b c", k=2, b=GR)
        b3h = e[:, 1, :].rearrange("p (k b c) -> p k b c", k=2, b=GR)
        b2s = y[:, 0, :].rearrange("p (k b c) -> p k b c", k=2, b=GR)
        xb = y[:, 1, :].rearrange("p (k b c) -> p k b c", k=2, b=GR)
        sm = sb("sm", [128, GR])
        vs = sb("vs", [128, 2, GR])
        rs = sb("rs", [128, 2, GR])
        b1s = t[:, 0:512].rearrange("p (b c) -> p b c", b=GR)
        v = junk[:, 0:512].rearrange("p (b c) -> p b c", b=GR)
        sq = junk[:, 512:1024].rearrange("p (b c) -> p b c", b=GR)
        xc = t[:, 512:1024].rearrange("p (b c) -> p b c", b=GR)

        E = ce[:, :].bitcast(bf16).rearrange("p (c u m) -> p c u m", c=KCH, u=UB)
        kbias = cf[:, 0:1]
        ident = cf[:, 1:129]
        fold2 = cf[:, 129:193]
        ncap = cf[:, 193:321]
        e0, t0, h0, tq, phi0 = (cols[:, n:n + 1] for n in range(5))
        adj_o = adj.rearrange("b (o r i) j -> b o r i j", r=OCT, i=2)
        VG = PR[:, 0:OCT, :]
        LNP = V[:, :, :].rearrange("p a n -> p (a n)").rearrange("p (b i) -> p b i", b=B)

        Z0 = pb("Z0", [128, UC])
        Z1 = pb("Z1", [128, UC])
        Z2 = pb("Z2", [128, UC])
        PTP = pb("PTP", [128, UC], bf16)
        PM = pb("PM", [128, 512])

        QF = [Z0[:, 512 * k:512 * k + 512].rearrange("p (b c) -> p b c", b=GR) for k in range(2)]
        QT = Z1[:, 0:512].rearrange("p (b i) -> p b i", b=GR // 2)
        Q3 = Z1[:, 512:1024].rearrange("p (b c) -> p b c", b=GR)
        Q2 = Z2[:, 0:512].rearrange("p (b c) -> p b c", b=GR)
        Q1 = Z2[:, 512:1024].rearrange("p (b c) -> p b c", b=GR)
        QO = PM[:, :].rearrange("p (b c) -> p b c", b=GR)

        names = """s_adjv s_adjn s_x s_cst s_w s_zero s_ones s_ident s_setA s_setP s_setD
                   s_arg s_e s_z1 s_t s_h s_z2 s_y s_p s_run s_mx s_mr s_sorted s_gath s_split
                   s_gp s_ptt s_pt s_deg s_d s_stage s_ltt s_ltev s_lt s_chk s_flp s_fl
                   s_lnp s_fold s_v s_ln s_x1 s_xt s_xte s_b3 s_b3e s_b2 s_b2e s_b1 s_b1e s_o s_fin s_out
                   s_rs s_gx s_ch s_gch g_load g_d g_split g_tr g_pt g_arg g_e g_z g_zb g_sp g_ab g_t g_l g_h g_acc g_ch g_parts s_parts g_done
                   s_vs s_b3h s_xb s_op""".split()
        S = {n: sem(n) for n in names}
        s_adjv = [sem(f"s_adjv{k}") for k in range(OCTETS)]
        s_adjn = [sem(f"s_adjn{k}") for k in range(8)]

        block = ctx.enter_context(nc.Block())

        @block.sync
        def _(sp):
            for n, o in enumerate(ORDER):
                for i2 in range(2):
                    src = adj[:, 16 * o + i2:16 * o + 16:2, :]
                    sp.dma_start(V[64 * i2:64 * i2 + 64, OCT * o:OCT * o + OCT, :], src)\
                        .then_inc(s_adjv[n], 16)
                if n == 0:
                    sp.dma_start(ce[0:KROWS, :], c_e).then_inc(S["s_cst"], 16)
                    sp.dma_start(cf[:, :], c_f).then_inc(S["s_cst"], 16)
            for g in range(8):
                sp.dma_start(LT[:, 8 * g:8 * g + 8, :], adj[8 * g:8 * g + 8, :, :].rearrange("b i j -> i b j"))\
                    .then_inc(s_adjn[g], 16)
            sp.wait_ge(S["s_fl"], 1)
            general = sp.value_load(flag[0:1, 0:1])
            with sp.If(general != 0):
                with sp.Fori(0, OCTETS) as o:
                    sp.wait_ge(S["g_acc"], GSTEPS * GBLK * o + 1)
                    for i2 in range(2):
                        sp.dma_start(VG[64 * i2:64 * i2 + 64, :, :], adj_o[:, o, :, i2, :])\
                            .then_inc(S["g_load"], 16)
            for g in range(8):
                sp.wait_ge(S["s_fin"], g + 1)
                sp.dma_start(out[8 * g:8 * g + 8, :, :].rearrange("b i c -> i b c"), X[:, 8 * g:8 * g + 8, :])\
                    .then_inc(S["s_out"], 16)
            sp.wait_ge(S["s_out"], 8 * 16)

        @block.scalar
        def _(act):
            act.preload_act_table_set("natural_log_exp_and_others")
            act.wait_ge(S["s_zero"], 1)
            for c in range(KCH):
                k = min(64, NRBF - 64 * c)
                for a in range(2):
                    act.dma_start(w1bd[64 * a:64 * a + k, c, 64 * a:64 * a + 64], W1[64 * c:64 * c + k, :])\
                        .then_inc(S["s_w"], 16)
            for a in range(2):
                act.dma_start(w2bd[64 * a:64 * a + 64, 64 * a:64 * a + 64], W2).then_inc(S["s_w"], 16)
                act.dma_start(b1c[64 * a:64 * a + 64, :], b1.rearrange("(f a) -> f a", a=1)).then_inc(S["s_w"], 16)
                act.dma_start(b2c[64 * a:64 * a + 64, :], b2.rearrange("(f a) -> f a", a=1)).then_inc(S["s_w"], 16)
                act.dma_start(wl[64 * a:64 * a + 64, :, 64 * a:64 * a + 64], WL.rearrange("k a c o -> (a c) k o"))\
                    .then_inc(S["s_w"], 16)
            act.dma_start(biasr[:, :], biasL.rearrange("a b o -> (a b) o").broadcast_to([128, F]))\
                .then_inc(S["s_w"], 16)
            act.dma_start(X[:, :, :], x.rearrange("b i c -> i b c")).then_inc(S["s_x"], 16)

            act.wait_ge(S["s_cst"], 32)
            act.wait_ge(S["s_w"], 15 * 16)
            nc.scalar.activation(e0, kbias, ACT.Exp).then_inc(S["s_setA"], 1)
            act.wait_ge(S["s_setP"], 3)
            nc.scalar.activation(t0, PM[:, 2:3], ACT.Exp, bias=b1c[:, :]).then_inc(S["s_setA"], 1)
            act.wait_ge(S["s_setA"], 2)
            nc.scalar.activation(h0, t0, ACT.Ln, bias=1.0).then_inc(S["s_setA"], 1)
            act.wait_ge(S["s_setP"], 4)
            act.wait_ge(S["s_setD"], 3)
            nc.scalar.activation(tq, PM[:, 3:4], ACT.Exp, bias=b2p[:, :]).then_inc(S["s_setA"], 1)
            act.wait_ge(S["s_setA"], 4)
            nc.scalar.activation(phi0, tq, ACT.Ln, bias=1.0).then_inc(S["s_setA"], 1)

            def exp_rbf(q, k):
                act.wait_ge(S["s_arg"], q + 1)
                nc.scalar.activation(e[:, k, :], Z0[:, :], ACT.Exp).then_inc(S["s_e"], 1)

            def exp_z1(q, k):
                act.wait_ge(S["s_z1"], q + 1)
                act.wait_ge(S["s_h"], q) if not isinstance(q, int) or q else None
                nc.scalar.activation(t[:, :], Z1[:, :], ACT.Exp, bias=b1c[:, :]).then_inc(S["s_t"], 1)

            def ln_z1(q, k):
                act.wait_ge(S["s_t"], q + 1)
                nc.scalar.activation(h[:, k, :], t[:, :], ACT.Ln, bias=1.0).then_inc(S["s_h"], 1)

            def exp_z2(q, k, wait=True):
                act.wait_ge(S["s_z2"], q + 1)
                if wait:
                    act.wait_ge(S["s_p"], q - 1)
                nc.scalar.activation(y[:, k, :], Z2[:, :], ACT.Exp, bias=b2p[:, :]).then_inc(S["s_y"], 1)

            exp_rbf(0, 0)
            exp_rbf(1, 1)
            exp_z1(0, 0)
            ln_z1(0, 0)
            for q in (2, 3):
                exp_rbf(q, q % 2)
                exp_z1(q - 1, (q - 1) % 2)
                exp_z2(q - 2, q % 2, wait=False)
                ln_z1(q - 1, (q - 1) % 2)
            with act.Fori(2, UNITS // 2) as m:
                for k in range(2):
                    exp_rbf(2 * m + k, k)
                    exp_z1(2 * m + k - 1, 1 - k)
                    exp_z2(2 * m + k - 2, k)
                    ln_z1(2 * m + k - 1, 1 - k)
            exp_z1(UNITS - 1, 1)
            exp_z2(UNITS - 2, 0)
            ln_z1(UNITS - 1, 1)
            exp_z2(UNITS - 1, 1)

            act.wait_ge(S["s_p"], UNITS)
            for o in range(OCTETS):
                nc.scalar.activation(LNP[:, :, 16 * o:16 * o + 16].rearrange("p b i -> p i b"),
                                     PR[:, OCT * o:OCT * o + OCT, :].rearrange("p t (i b) -> p (t i) b", i=2),
                                     ACT.Ln).then_inc(S["s_lnp"], 1)

            act.wait_ge(S["s_fl"], 1)
            general = act.value_load(flag[0:1, 0:1])
            with act.If(general != 0):
                with act.Fori(0, OCTETS * GBLK * GSTEPS) as m:
                    for c in range(KCH):
                        act.wait_ge(S["g_arg"], KCH * m + c + 1)
                        nc.scalar.activation(e[:, 0, :], Z0[:, :], ACT.Exp).then_inc(S["g_e"], 1)
                    for layer in range(2):
                        act.wait_ge(S["g_ab"], 2 * m + layer + 1)
                        nc.scalar.activation(t[:, :], y[:, 0, :], ACT.Exp, scale=-1.0).then_inc(S["g_t"], 1)
                        act.wait_ge(S["g_t"], 2 * m + layer + 1)
                        nc.scalar.activation(h[:, 1, :], t[:, :], ACT.Ln, bias=1.0).then_inc(S["g_l"], 1)
                act.wait_ge(S["g_done"], 1)

            for g in range(8):
                k = g % 2
                act.wait_ge(S["s_xt"], g + 1)
                nc.scalar.activation(x1t[:, k, :, :], QT, ACT.Copy).then_inc(S["s_xte"], 1)
                act.wait_ge(S["s_b3"], g + 1)
                nc.scalar.activation(b3s[:, k, :, :], Q3, ACT.Copy).then_inc(S["s_b3e"], 1)
                act.wait_ge(S["s_b2"], g + 1)
                if g >= 2:
                    act.wait_ge(S["s_xb"], g - 1)
                nc.scalar.activation(b2s[:, k, :, :], Q2, ACT.Copy).then_inc(S["s_b2e"], 1)

        @block.tensor
        def _(pe):
            def mm(o, w, r, start=True, stop=True):
                return nc.tensor.matmul(o, w, r, start=start, stop=stop)

            pe.wait_ge(S["s_w"], 15 * 16)
            pe.wait_ge(S["s_setD"], 2)
            mm(PM[:, 0:1], w2bd[:, :], nl2[:, :]).then_inc(S["s_setP"], 1)
            mm(PM[:, 1:2], w1abs[:, :], onec[:, :]).then_inc(S["s_setP"], 1)
            pe.wait_ge(S["s_setA"], 1)
            pe.wait_ge(S["s_setD"], 4)
            mm(PM[:, 2:3], w1bd[:, 0, :], e0).then_inc(S["s_setP"], 1)
            pe.wait_ge(S["s_setA"], 3)
            mm(PM[:, 3:4], w2bd[:, :], h0).then_inc(S["s_setP"], 1)
            pe.wait_ge(S["s_setD"], 5)
            mm(PM[:, 64:128], ncap[0:64, :], diag[:, :]).then_inc(S["s_setP"], 1)

            def args(q, u, k, first=False):
                if not first:
                    pe.wait_ge(S["s_e"], q)
                for c in range(2):
                    last = mm(Z0[:, 512 * c:512 * c + 512], E[0:KROWS, 0, u, :],
                              PT[0:KROWS, k, 512 * c:512 * c + 512])
                last.then_inc(S["s_arg"], 1)

            def layer1(q, u):
                pe.wait_ge(S["s_e"], q + 1)
                pe.wait_ge(S["s_t"], q)
                for c in range(2):
                    last = mm(Z1[:, 512 * c:512 * c + 512], w1bd[:, 0, :], e[:, u % 2, 512 * c:512 * c + 512])
                last.then_inc(S["s_z1"], 1)

            def layer2(q, u):
                pe.wait_ge(S["s_h"], q + 1)
                pe.wait_ge(S["s_y"], q)
                for c in range(2):
                    last = mm(Z2[:, 512 * c:512 * c + 512], w2bd[:, :], h[:, u % 2, 512 * c:512 * c + 512])
                last.then_inc(S["s_z2"], 1)

            def transpose_block(bk, k):
                pe.wait_ge(S["s_split"], bk + 1)
                for r in range(OCT):
                    last = nc.tensor.transpose(PTP[0:PROWS, 128 * r:128 * r + 128], BUF[:, k, r, :], identb[:, :])
                last.then_inc(S["s_ptt"], 1)

            def transpose_lap(n, k):
                pe.wait_ge(S["s_stage"], n + 1)
                pe.wait_ge(S["s_ltev"], n)
                for g in range(4):
                    last = nc.tensor.transpose(PM[:, 128 * g:128 * g + 128], stage[:, k, g, :], ident)
                last.then_inc(S["s_ltt"], 1)

            pe.wait_ge(S["s_ident"], 2)
            pe.wait_ge(S["s_ones"], 1)
            transpose_block(0, 0)
            pe.wait_ge(S["s_pt"], 1)
            args(0, 0, 0, first=True)

            def block_body(bk, k, first=False, last=False, lap=True):
                for u in range(UB):
                    q = UB * bk + u
                    if lap and u in (1, 5):
                        transpose_lap(2 * (bk - 1) + (u == 5), int(u == 5))
                    if u == 4 and not last:
                        transpose_block(bk + 1, 1 - k)
                    if not (first and u < 2):
                        layer2(q - 2, u)
                    if u < UB - 1:
                        args(q + 1, u + 1, k)
                    elif not last:
                        pe.wait_ge(S["s_pt"], bk + 2)
                        args(q + 1, 0, 1 - k)
                    layer1(q, u)

            block_body(0, 0, first=True, lap=False)
            pe.wait_ge(S["s_setD"], 6)
            for bk in range(1, 9):
                block_body(bk, bk % 2)
            block_body(NBLK - 1, (NBLK - 1) % 2, last=True, lap=False)
            layer2(UNITS - 2, 0)
            layer2(UNITS - 1, 1)

            pe.wait_ge(S["s_chk"], 1)
            mm(PM[0:1, 0:1], flagc[:, 7:8], onec[:, :]).then_inc(S["s_flp"], 1)

            pe.wait_ge(S["s_lnp"], OCTETS)
            pe.wait_ge(S["s_lt"], LTB)
            pe.wait_ge(S["s_fl"], 1)
            general = pe.value_load(flag[0:1, 0:1])
            with pe.If(general != 0):
                with pe.Fori(0, OCTETS * GBLK) as n:
                    pe.wait_ge(S["g_split"], n + 1)
                    for r in range(OCT):
                        last = nc.tensor.transpose(PTP[0:PROWS, 128 * r:128 * r + 128], BUF[:, 0, r, :], identb[:, :])
                    last.then_inc(S["g_tr"], 1)
                    pe.wait_ge(S["g_pt"], n + 1)
                    for u in range(GSTEPS):
                        m = GSTEPS * n + u
                        pe.wait_ge(S["g_acc"], m + 1)
                        for c in range(KCH):
                            if c:
                                pe.wait_ge(S["g_e"], KCH * m + c)
                            for a in range(2):
                                last = mm(Z0[:, 512 * a:512 * a + 512], E[0:KROWS, c, u, :],
                                          PT[0:KROWS, 0, 512 * a:512 * a + 512])
                            last.then_inc(S["g_arg"], 1)
                            pe.wait_ge(S["g_e"], KCH * m + c + 1)
                            for a in range(2):
                                last = mm(Z1[:, 512 * a:512 * a + 512], w1bd[:, c, :], e[:, 0, 512 * a:512 * a + 512],
                                          start=c == 0, stop=c == KCH - 1)
                        last.then_inc(S["g_z"], 1)
                        pe.wait_ge(S["g_h"], m + 1)
                        for a in range(2):
                            last = mm(Z2[:, 512 * a:512 * a + 512], w2bd[:, :], h[:, 0, 512 * a:512 * a + 512])
                        last.then_inc(S["g_z"], 1)
                pe.wait_ge(S["g_done"], 1)

            def fold(g):
                if g >= 2:
                    pe.wait_ge(S["s_v"], g - 1)
                for b in range(GR):
                    last = mm(QF[g % 2][:, b, :], LNP[:, GR * g + b, :], fold2)
                last.then_inc(S["s_fold"], 1)

            def terms(o, g, w, other=None):
                if other is None:
                    for b in range(0, GR, 2):
                        last = mm(o[:, b:b + 2, :], x1t[:, g % 2, b // 2, :], wl[:, w, :])
                    return last
                for b in range(GR):
                    a = 64 * (b % 2)
                    mm(o[:, b, :], x1t[:, g % 2, b // 2, :], wl[:, w, a:a + 64], stop=False)
                    last = mm(o[:, b, :], LT[:, GR * g + b, :], other[:, b, :], start=False)
                return last

            fold(0)
            for g in range(9):
                if g + 1 < 8:
                    fold(g + 1)
                if g >= 1:
                    pe.wait_ge(S["s_b2e"], g)
                    pe.wait_ge(S["s_b1e"], g - 1) if g >= 2 else None
                    terms(Q1, g - 1, 1, b2s[:, (g - 1) % 2, :, :]).then_inc(S["s_b1"], 1)
                if g < 8:
                    pe.wait_ge(S["s_x1"], g + 1)
                    for b in range(0, GR, 2):
                        last = nc.tensor.transpose(QT[:, b // 2, :],
                                                   x1s[:, g % 2, b:b + 2, :].rearrange("p b c -> p (b c)"), ident)
                    last.then_inc(S["s_xt"], 1)
                if g >= 1:
                    pe.wait_ge(S["s_b1e"], g)
                    pe.wait_ge(S["s_o"], g - 1) if g >= 2 else None
                    terms(QO, g - 1, 0, b1s).then_inc(S["s_op"], 1)
                if g < 8:
                    pe.wait_ge(S["s_xte"], g + 1)
                    terms(Q3, g, 3).then_inc(S["s_b3"], 1)
                    pe.wait_ge(S["s_b3e"], g + 1)
                    terms(Q2, g, 2, b3s[:, g % 2, :, :]).then_inc(S["s_b2"], 1)

        @block.vector
        def _(dve):
            V_ = nc.vector
            chain = [0]

            def link(ins):
                chain[0] += 1
                ins.then_inc(S["s_ch"], 1)
                dve.wait_ge(S["s_ch"], chain[0])

            V_.memset(nl2[:, :], -LOG2)
            V_.memset(PT[ONES:KROWS, :, :], 1.0).then_inc(S["s_ones"], 1)
            V_.memset(onec[:, :], 1.0).then_inc(S["s_setD"], 1)
            dve.wait_ge(S["s_cst"], 32)
            V_.tensor_copy(identb[:, :], ident).then_inc(S["s_ident"], 1)
            V_.tensor_scalar(ident2[:, :], ident, 2.0, None, ALU.mult).then_inc(S["s_ident"], 1)

            def sort(first):
                if first % OCT == 0:
                    dve.wait_ge(s_adjv[first // OCT], 32)
                pair = [OCT * ORDER[n // OCT] + n % OCT for n in (first, first + 1)]
                rounds = max(-(-CAPS[a] // 8) for a in pair)
                for k in range(rounds):
                    for a in pair:
                        last = V_.max(SRT[:, a, 8 * k:8 * k + 8], V[:, a, :])
                    if k < rounds - 1:
                        link(last)
                        for a in pair:
                            mr = V_.match_replace(V[:, a, :], SRT[:, a, 8 * k:8 * k + 8], V[:, a, :], 0.0)
                        link(mr)
                last.then_inc(S["s_sorted"], 1)

            for n in range(0, OCT, 2):
                sort(n)
            dve.wait_ge(S["s_w"], 15 * 16)
            V_.scalar_tensor_tensor(w1abs[:, :], w1bd[:, 0, :], -1.0, w1bd[:, 0, :], ALU.mult, ALU.max).then_inc(S["s_setD"], 1)
            dve.wait_ge(S["s_setP"], 2)
            V_.tensor_tensor(b2p[:, :], PM[:, 0:1], b2c[:, :], ALU.add).then_inc(S["s_setD"], 1)
            link(V_.scalar_tensor_tensor(zc[:, 0:1], b1c[:, :], -1.0, b1c[:, :], ALU.mult, ALU.max))
            V_.tensor_tensor(zc[:, 1:2], PM[:, 1:2], zc[:, 0:1], ALU.add).then_inc(S["s_setD"], 1)
            dve.wait_ge(S["s_setA"], 5)
            V_.tensor_scalar(diag[:, :], ident[0:64, 0:64], phi0[0:64, :], None, ALU.mult).then_inc(S["s_setD"], 1)
            dve.wait_ge(S["s_setP"], 5)
            V_.tensor_scalar(C1[:, :], PM[:, 64:128], 1.0 - N * LOG2, None, ALU.add).then_inc(S["s_setD"], 1)

            def evac_block(bk):
                dve.wait_ge(S["s_ptt"], bk + 1)
                if bk >= 2:
                    dve.wait_ge(S["s_arg"], UB * (bk - 1))
                V_.tensor_copy(PT[0:PROWS, bk % 2, :], PTP[0:PROWS, :]).then_inc(S["s_pt"], 1)

            def evac_lap(n):
                dve.wait_ge(S["s_ltt"], n + 1)
                dve.wait_ge(S["s_d"], 1)
                V_.tensor_tensor(LT[:, 4 * n:4 * n + 4, :], PM[:, :].rearrange("p (g i) -> p g i", g=4),
                                 dinv[:, 4 * n:4 * n + 4].unsqueeze(2).broadcast_to([128, 4, 128]), ALU.mult)\
                    .then_inc(S["s_ltev"], 1)

            evac_block(0)
            for n in range(OCT, SORT_AHEAD, 2):
                sort(n)
            runs_done = 0
            for bk in range(NBLK):
                for u in range(UB):
                    q = UB * bk + u
                    if u == 2 and bk + 1 < NBLK:
                        evac_block(bk + 1)
                    if 1 <= bk <= 8 and u in (1, 5):
                        evac_lap(2 * (bk - 1) + (u == 5))
                    if bk == 0:
                        dve.wait_ge(s_adjn[u], 16)
                        grp = LT[:, 8 * u:8 * u + 8, :]
                        V_.tensor_reduce(deg[:, 8 * u:8 * u + 8], grp, AX.X, ALU.add).then_inc(S["s_deg"], 1)
                        V_.tensor_scalar(junk[:, :], grp.rearrange("p b j -> p (b j)"), 0.0, 0.0, ALU.is_equal, ALU.add,
                                         accum_out=okz[:, u:u + 1])
                    if SORT_AHEAD + 2 * q < TILES:
                        sort(SORT_AHEAD + 2 * q)
                    dve.wait_ge(S["s_y"], q + 1)
                    pieces = runs_of_unit(q)
                    if not pieces:
                        V_.memset(junk[:, 0:1], 0.0).then_inc(S["s_p"], 1)
                    for n, (r, live, tile, fresh, o) in enumerate(pieces):
                        src = y[:, q % 2, 128 * r:128 * (r + live)].rearrange("p (t m) -> p t m", m=128)
                        dst = PR[:, tile:tile + live, :]
                        if runs_done:
                            dve.wait_ge(S["s_run"], runs_done)
                        if fresh:
                            ins = V_.tensor_scalar(dst, src, 1.0, None, ALU.add)
                        else:
                            ins = V_.scalar_tensor_tensor(dst, src, 1.0, dst, ALU.add, ALU.mult)
                        ins.then_inc(S["s_run"], 1)
                        runs_done += 1
                    if pieces:
                        dve.wait_ge(S["s_run"], runs_done)
                        V_.sem_inc(S["s_p"], 1)

            dve.wait_ge(S["s_gath"], 1)
            link(V_.tensor_scalar(junk[:, :], D[:, 0:512, :].rearrange("p f s -> p (f s)"), 0.0, 0.0, ALU.is_equal,
                                  ALU.add, accum_out=okz[:, 8:9]))
            link(V_.tensor_scalar(junk[:, 0:2 * (NBLK * BI - 512)], D[:, 512:, :].rearrange("p f s -> p (f s)"),
                                  0.0, 0.0, ALU.is_equal, ALU.add, accum_out=okz[:, 9:10]))
            V_.tensor_reduce(flagc[:, 0:1], D[:, :, :], AX.XY, ALU.max)
            V_.tensor_reduce(flagc[:, 1:2], okz[:, 0:8], AX.X, ALU.add)
            V_.tensor_reduce(flagc[:, 2:3], okz[:, 8:10], AX.X, ALU.add)
            V_.tensor_reduce(zc[:, 2:3], PR[:, :, :], AX.XY, ALU.max)
            link(V_.tensor_reduce(zc[:, 3:4], PR[:, :, :], AX.XY, ALU.min))
            link(V_.tensor_tensor(flagc[:, 3:4], flagc[:, 2:3], flagc[:, 1:2], ALU.subtract))
            link(V_.tensor_scalar(flagc[:, 0:1], flagc[:, 0:1], DMAX, None, ALU.is_le))
            link(V_.scalar_tensor_tensor(flagc[:, 4:5], zc[:, 1:2], ZMAX, flagc[:, 0:1], ALU.is_le, ALU.add))
            link(V_.scalar_tensor_tensor(flagc[:, 5:6], zc[:, 2:3], PMAX, flagc[:, 4:5], ALU.is_le, ALU.add))
            link(V_.scalar_tensor_tensor(flagc[:, 6:7], zc[:, 3:4], 1.0, flagc[:, 5:6], ALU.is_ge, ALU.add))
            link(V_.tensor_tensor(flagc[:, 7:8], flagc[:, 3:4], flagc[:, 6:7], ALU.subtract))
            link(V_.tensor_scalar(flagc[:, 7:8], flagc[:, 7:8], float(4 + B * N - 2 * NBLK * BI), None, ALU.add))
            V_.sem_inc(S["s_chk"], 1)
            dve.wait_ge(S["s_flp"], 1)
            V_.tensor_copy(flag[:, :], PM[0:1, 0:1]).then_inc(S["s_fl"], 1)

            dve.wait_ge(S["s_fl"], 1)
            general = dve.value_load(flag[0:1, 0:1])
            with dve.If(general != 0):
                dve.wait_ge(S["s_lnp"], OCTETS)
                V_.memset(V[:, :, :], 0.0).then_inc(S["g_acc"], 1)
                with dve.Fori(0, OCTETS) as o:
                    with dve.Fori(0, GBLK) as c:
                        n = GBLK * o + c
                        dve.wait_ge(S["g_load"], 32 * o + 32)
                        rows = VG.rearrange("p r (c u s) -> p c u r s", c=GBLK, u=UB)
                        V_.tensor_copy(D[:, 0:BI, :].rearrange("p (u r) s -> p u r s", u=UB), rows[:, c])\
                            .then_inc(S["g_d"], 1)
                        dve.wait_ge(S["g_tr"], n + 1)
                        V_.tensor_copy(PT[0:PROWS, 0, :], PTP[0:PROWS, :]).then_inc(S["g_pt"], 1)
                        with dve.Fori(0, GSTEPS) as u:
                            m = GSTEPS * n + u
                            for layer, (z, bias) in enumerate(((Z1, b1c), (Z2, b2p))):
                                dve.wait_ge(S["g_z"], 2 * m + layer + 1)
                                V_.tensor_scalar(junk[:, :], z[:, :], bias[:, :], None, ALU.add)\
                                    .then_inc(S["g_zb"], 1)
                                dve.wait_ge(S["g_zb"], 2 * m + layer + 1)
                                V_.scalar_tensor_tensor(y[:, 0, :], junk[:, :], -1.0, junk[:, :], ALU.mult, ALU.max)\
                                    .then_inc(S["g_ab"], 1)
                                dve.wait_ge(S["g_l"], 2 * m + layer + 1)
                                V_.scalar_tensor_tensor(h[:, 0, :], junk[:, :], 0.0, h[:, 1, :], ALU.max, ALU.add)\
                                    .then_inc(S["g_sp"], 1)
                                dve.wait_ge(S["g_sp"], 2 * m + layer + 1)
                                if layer == 0:
                                    dve.sem_inc(S["g_h"], 1)
                            sums = LNP.rearrange("p b (o i) -> p o i b", o=OCTETS)[:, o]
                            dve.wait_ge(S["g_acc"], m + 1)
                            V_.tensor_tensor(sums, sums, h[:, 0, :].rearrange("p (i b) -> p i b", b=B), ALU.add)\
                                .then_inc(S["g_acc"], 1)
                V_.memset(C1[:, :], 1.0 - N * LOG2).then_inc(S["g_done"], 1)
                dve.wait_ge(S["g_done"], 1)

            def norm(src, dst, k, n):
                link(V_.tensor_reduce(sm[:, :], src, AX.X, ALU.add))
                link(V_.scalar_tensor_tensor(xc, sm[:, :].unsqueeze(2).broadcast_to([128, GR, F]), -1.0 / F, src,
                                             ALU.mult, ALU.add))
                link(V_.tensor_tensor(sq, xc, xc, ALU.mult))
                V_.tensor_reduce(vs[:, k, :], sq, AX.X, ALU.add).then_inc(S["s_vs"], 1)
                dve.wait_ge(S["s_rs"], n)
                return V_.tensor_tensor(dst, xc, rs[:, k, :].unsqueeze(2).broadcast_to([128, GR, F]), ALU.mult)

            norms = [0]

            def ln1(g):
                dve.wait_ge(S["s_fold"], g + 1)
                ins = V_.tensor_tensor(v, QF[g % 2], C1[:, :].unsqueeze(1).broadcast_to([128, GR, F]), ALU.add)
                ins.then_inc(S["s_v"], 1)
                dve.wait_ge(S["s_v"], g + 1)
                link(V_.tensor_tensor(v, v, X[:, GR * g:GR * g + GR, :], ALU.mult))
                norms[0] += 1
                if g >= 2:
                    dve.wait_ge(S["s_xb"], g - 1)
                norm(v, x1s[:, g % 2, :, :], 0, norms[0]).then_inc(S["s_x1"], 1)

            def ln2(g):
                dve.wait_ge(S["s_op"], g + 1)
                dve.wait_ge(S["s_xb"], g + 1)
                ins = V_.tensor_tensor(v, QO, xb[:, g % 2, :, :], ALU.add)
                ins.then_inc(S["s_o"], 1)
                dve.wait_ge(S["s_o"], g + 1)
                norms[0] += 1
                norm(v, X[:, GR * g:GR * g + GR, :], 1, norms[0]).then_inc(S["s_fin"], 1)

            dve.wait_ge(S["s_x"], 16)
            ln1(0)
            for g in range(9):
                if g >= 1:
                    dve.wait_ge(S["s_b1"], g)
                    dve.wait_ge(S["s_b3h"], g)
                    V_.scalar_tensor_tensor(b1s, Q1, 0.5, b3h[:, (g - 1) % 2, :, :], ALU.mult, ALU.subtract)\
                        .then_inc(S["s_b1e"], 1)
                if g + 1 < 8:
                    ln1(g + 1)
                if g >= 1:
                    ln2(g - 1)

        @block.gpsimd
        def _(pool):
            G = nc.gpsimd
            G.memset(w1bd[:, :, :], 0.0)
            G.memset(w2bd[:, :], 0.0)
            G.memset(wl[:, :, :], 0.0)
            G.memset(D[:, ITEMS:, :], 0.0)
            G.memset(mhalf[:, :], -0.5).then_inc(S["s_zero"], 1)
            chain = [0]

            def link(ins):
                chain[0] += 1
                ins.then_inc(S["s_gch"], 1)
                pool.wait_ge(S["s_gch"], chain[0])

            def gather(bk):
                for o, lev, live, at in LEVELS:
                    if BI * bk <= at < BI * bk + BI:
                        pool.wait_ge(S["s_sorted"], OCT // 2 * (ORDER.index(o) + 1))
                        last = G.tensor_copy(D[:, at:at + live, :],
                                             SRT[:, OCT * o:OCT * o + live, 2 * lev:2 * lev + 2])
                return last

            def block_views(k, first):
                shape = "p (u r) s -> p u r s"
                return (BUF[:, k, :, :].rearrange("p r (u a s) -> p a u r s", u=UB, a=PARTS),
                        D[:, first:first + BI, :].rearrange(shape, u=UB), dd[:, :, :].rearrange(shape, u=UB),
                        r1[:, :, :].rearrange(shape, u=UB), dl[:, :, :].rearrange(shape, u=UB))

            def first_parts(part, dist, square, rest, rest2):
                G.tensor_tensor(square, dist, dist, ALU.mult)
                G.tensor_copy(part[:, 0], dist)
                return G.tensor_tensor(part[:, 3], dist, dist, ALU.mult)

            def second_parts(part, dist, square, rest, rest2):
                G.tensor_tensor(rest, dist, part[:, 0], ALU.subtract)
                G.tensor_tensor(part[:, 1], dist, part[:, 0], ALU.subtract)
                G.tensor_tensor(rest2, square, part[:, 3], ALU.subtract)
                return G.tensor_tensor(part[:, 4], square, part[:, 3], ALU.subtract)

            def third_parts(part, dist, square, rest, rest2):
                G.tensor_tensor(part[:, 2], rest, part[:, 1], ALU.subtract)
                return G.tensor_tensor(part[:, 5], rest2, part[:, 4], ALU.subtract)

            def split(bk):
                if bk >= 2:
                    pool.wait_ge(S["s_ptt"], bk - 1)
                if bk:
                    pool.wait_ge(S["s_split"], bk)
                views = block_views(bk % 2, BI * bk)
                first_parts(*views).then_inc(S["s_parts"], 1)
                pool.wait_ge(S["s_parts"], 2 * bk + 1)
                second_parts(*views).then_inc(S["s_parts"], 1)
                pool.wait_ge(S["s_parts"], 2 * bk + 2)
                third_parts(*views).then_inc(S["s_split"], 1)

            def scale_rows(n):
                if n >= 2:
                    pool.wait_ge(S["s_ltt"], n - 1)
                G.tensor_tensor(stage[:, n % 2, :, :], LT[:, 4 * n:4 * n + 4, :],
                                dinv2[:, 4 * n:4 * n + 4].unsqueeze(2).broadcast_to([128, 4, 128]), ALU.mult)\
                    .then_inc(S["s_stage"], 1)

            def add_diagonal(n):
                if n:
                    pool.wait_ge(S["s_lt"], n)
                link(G.tensor_tensor(ie[:, :, :], ident2[:, :].unsqueeze(1).broadcast_to([128, 4, 128]),
                                     enz[:, 4 * n:4 * n + 4].unsqueeze(2).broadcast_to([128, 4, 128]), ALU.mult))
                pool.wait_ge(S["s_ltev"], n + 1)
                G.tensor_tensor(LT[:, 4 * n:4 * n + 4, :], LT[:, 4 * n:4 * n + 4, :], ie[:, :, :], ALU.add)\
                    .then_inc(S["s_lt"], 1)

            link(gather(0))
            split(0)
            link(gather(1))
            split(1)
            pool.wait_ge(S["s_deg"], 8)
            pool.wait_ge(S["s_ident"], 2)
            G.tensor_scalar(enz[:, :], deg[:, :], 0.0, None, ALU.is_equal)
            G.tensor_scalar(dinv2[:, :], deg[:, :], 0.0, None, ALU.is_gt)
            link(G.tensor_scalar(dinv[:, :], deg[:, :], 1.2e-38, None, ALU.max))
            link(G.tensor_tensor(dinv[:, :], dinv[:, :], mhalf[:, :], ALU.pow))
            link(G.tensor_scalar(enz[:, :], enz[:, :], -1.0, 1.0, ALU.mult, ALU.add))
            link(G.tensor_tensor(dinv[:, :], dinv[:, :], dinv2[:, :], ALU.mult))
            G.tensor_scalar(dinv2[:, :], dinv[:, :], -2.0, None, ALU.mult).then_inc(S["s_d"], 1)
            pool.wait_ge(S["s_d"], 1)
            for bk in range(1, NBLK):
                if bk + 1 < NBLK:
                    link(gather(bk + 1))
                    if bk + 1 == NBLK - 1:
                        G.sem_inc(S["s_gath"], 1)
                    split(bk + 1)
                if bk <= 8:
                    scale_rows(2 * bk - 2)
                    scale_rows(2 * bk - 1)
                if 2 <= bk:
                    add_diagonal(2 * bk - 4)
                    add_diagonal(2 * bk - 3)

            pool.wait_ge(S["s_fl"], 1)
            general = pool.value_load(flag[0:1, 0:1])
            with pool.If(general != 0):
                with pool.Fori(0, OCTETS * GBLK) as n:
                    pool.wait_ge(S["g_d"], n + 1)
                    views = block_views(0, 0)
                    first_parts(*views).then_inc(S["g_parts"], 1)
                    pool.wait_ge(S["g_parts"], 2 * n + 1)
                    second_parts(*views).then_inc(S["g_parts"], 1)
                    pool.wait_ge(S["g_parts"], 2 * n + 2)
                    third_parts(*views).then_inc(S["g_split"], 1)
                pool.wait_ge(S["g_done"], 1)

            def root(n, k):
                pool.wait_ge(S["s_vs"], n)
                link(G.tensor_scalar(rs[:, k, :], vs[:, k, :], 1.0 / F, EPS, ALU.mult, ALU.add))
                G.tensor_tensor(rs[:, k, :], rs[:, k, :], mhalf[:, 0:GR], ALU.pow).then_inc(S["s_rs"], 1)

            root(1, 0)
            n = 1
            for g in range(9):
                if g >= 1:
                    k = (g - 1) % 2
                    pool.wait_ge(S["s_b3e"], g)
                    if g >= 3:
                        pool.wait_ge(S["s_b1e"], g - 2)
                        pool.wait_ge(S["s_o"], g - 2)
                    G.tensor_scalar(b3h[:, k, :, :], b3s[:, k, :, :], 0.5, None, ALU.mult).then_inc(S["s_b3h"], 1)
                if g >= 1:
                    link(G.tensor_tensor(xb[:, k, :, :], x1s[:, k, :, :],
                                         biasr[:, :].unsqueeze(1).broadcast_to([128, GR, F]), ALU.add))
                    pool.wait_ge(S["s_b2e"], g)
                    G.tensor_tensor(xb[:, k, :, :], xb[:, k, :, :], b2s[:, k, :, :], ALU.subtract)\
                        .then_inc(S["s_xb"], 1)
                if g + 1 < 8:
                    n += 1
                    root(n, 0)
                if g >= 1:
                    n += 1
                    root(n, 1)


def _bf16_bits(a):
    b = np.ascontiguousarray(a, np.float32).view(np.uint32).astype(np.uint64)
    return ((b + 0x7fff + ((b >> 16) & 1)) >> 16).astype(np.uint16)


def _constants():
    ce = np.zeros((KROWS, KCH, UB, 2, 64), np.float32)
    k = np.arange(64 * KCH).reshape(KCH, 64)
    for u in range(UB):
        for s in range(2):
            for a in range(PARTS):
                ce[(u * PARTS + a) * 2 + s, :, u, s, :] = 2 * k if a < 3 else -10.0
    rest = np.broadcast_to((-0.1 * k.astype(np.float64) ** 2)[:, None, None, :], (KCH, UB, 2, 64))
    bits = _bf16_bits(ce)
    for n in range(3):
        bits[ONES + n] = _bf16_bits(rest)
        rest = rest - (bits[ONES + n].astype(np.uint32) << 16).view(np.float32)
    cf = np.zeros((128, 1 + 128 + 64 + 128), np.float32)
    cf[:, 0] = -0.1 * (np.arange(128) % 64).astype(np.float64) ** 2
    cf[:, 1:129] = np.eye(128)
    cf[:, 129:193] = np.concatenate([np.eye(64), np.eye(64)])
    cf[:, 193:321] = N - np.repeat(np.array(CAPS), 2)
    return bits.reshape(KROWS, -1), cf


def kernel(x, adj, L0_gnn_W1, L0_gnn_b1, L0_gnn_W2, L0_gnn_b2, L1_gnn_weight, L1_gnn_bias):
    import concourse.bacc as bacc
    from concourse.bass_utils import run_bass_kernel_spmd

    nc = bacc.Bacc("TRN2", target_bir_lowering=False, num_devices=1)
    c_e, c_f = _constants()
    arrays, args = {}, []
    for name, a in (("x", x), ("adj", adj), ("W1", L0_gnn_W1), ("b1", L0_gnn_b1), ("W2", L0_gnn_W2),
                    ("b2", L0_gnn_b2), ("WL", L1_gnn_weight), ("biasL", L1_gnn_bias), ("c_e", c_e), ("c_f", c_f)):
        a = np.ascontiguousarray(a)
        arrays[f"in_{name}"] = a
        args.append(nc.dram_tensor(f"in_{name}", a.shape, mybir.dt.from_np(a.dtype), kind="ExternalInput").ap())
    out = nc.dram_tensor("out_y", (B, N, F), mybir.dt.float32, kind="ExternalOutput").ap()
    build(nc, *args, out)
    r = run_bass_kernel_spmd(nc, [arrays], core_ids=[0])
    return r.results[0]["out_y"]
```

```python
import numpy as np
import concourse.bass as bass
from concourse import mybir
from contextlib import ExitStack

B, N, F = 64, 128, 64
NRBF = 150
LOG2 = float(np.log(2.0))
EPS = 1e-5

TILES = N // 2
OCT = 8
OCTETS = TILES // OCT
CAPS = [56, 38, 34, 30, 28, 26, 24, 24, 24, 22, 22, 22, 20, 20, 20, 18,
        20, 18, 18, 18, 18, 18, 16, 16, 18, 18, 16, 16, 16, 16, 16, 16,
        16, 16, 16, 14, 14, 14, 14, 14, 14, 14, 14, 14, 14, 14, 14, 14,
        14, 14, 14, 14, 14, 14, 14, 12, 14, 14, 14, 14, 14, 14, 14, 12]
SLOTMAX = 64

ORDER = [3, 2, 4, 5, 6, 7, 1, 0]
LEVELS = []
ITEMS = 0
for o in ORDER:
    caps = CAPS[OCT * o:OCT * o + OCT]
    for lev in range(caps[0] // 2):
        live = sum(c > 2 * lev for c in caps)
        LEVELS.append((o, lev, live, ITEMS))
        ITEMS += live
UB = 8
BI = UB * OCT
NBLK = -(-ITEMS // BI)
assert ITEMS == NBLK * BI
UNITS = NBLK * UB
UC = OCT * 128
SORT_AHEAD = 16

PARTS = 6
PROWS = UB * 2 * PARTS
ONES = 96
KROWS = ONES + 3
KCH = 3
DMAX = 3.0
ZMAX = 40.0
PMAX = 2.0 ** 60
GBLK = N // (2 * UB)
GSTEPS = UB
LTB = 16
GR = 8


OCTET_END = {o: max(at + live for p, _, live, at in LEVELS if p == o) for o in ORDER}
DZ_ALL = 8 + 3 + OCTETS


def runs_of_unit(q):
    out = []
    for o, lev, live, at in LEVELS:
        a, b = max(at, OCT * q), min(at + live, OCT * q + OCT)
        if a < b:
            out.append((a - OCT * q, b - a, OCT * o + a - at, lev == 0, o))
    return out


def build(nc, x, adj, W1, b1, W2, b2, WL, biasL, c_e, c_f, out):
    f32, bf16, i32 = mybir.dt.float32, mybir.dt.bfloat16, mybir.dt.int32
    ALU = mybir.AluOpType
    ACT = mybir.ActivationFunctionType
    AX = mybir.AxisListType
    ctx = ExitStack()
    with ctx:
        def sb(name, shape, dt=f32):
            return ctx.enter_context(nc.sbuf_tensor(name, shape, dt))

        def pb(name, shape, dt=f32):
            return ctx.enter_context(nc.psum_tensor(name, shape, dt))

        def sem(name):
            return ctx.enter_context(nc.semaphore(name))

        V = sb("V", [128, TILES, N])
        LT = sb("LT", [128, B, N])
        PR = sb("PR", [128, TILES, 128])
        X = sb("X", [128, B, F])
        SRT = sb("SRT", [128, TILES, SLOTMAX])
        D = sb("D", [128, NBLK * BI, 2])
        BUF = sb("BUF", [128, 2, OCT, UB * 2 * PARTS], bf16)
        PT = sb("PT", [128, 2, UC], bf16)
        r1 = sb("r1", [128, BI, 2])
        dd = sb("dd", [128, BI, 2])
        dl = sb("dl", [128, BI, 2])
        e = sb("e", [128, 2, UC])
        t = sb("t", [128, UC])
        h = sb("h", [128, 2, UC])
        y = sb("y", [128, 2, UC])
        junk = sb("junk", [128, UC])
        ce = sb("ce", [128, KCH * UB * 128], mybir.dt.uint16)
        cf = sb("cf", [128, 1 + 128 + 64 + 128])
        identb = sb("identb", [128, 128], bf16)
        ident2 = sb("ident2", [128, 128])
        w1bd = sb("w1bd", [128, KCH, 128])
        w2bd = sb("w2bd", [128, 128])
        w1abs = sb("w1abs", [128, 128])
        b1c = sb("b1c", [128, 1])
        b2c = sb("b2c", [128, 1])
        b2p = sb("b2p", [128, 1])
        wl = sb("wl", [128, 4, 2 * F])
        biasr = sb("biasr", [128, F])
        cols = sb("cols", [128, 8])
        diag = sb("diag", [64, 64])
        C1 = sb("C1", [128, F])
        deg = sb("deg", [128, B])
        dinv = sb("dinv", [128, B])
        dinv2 = sb("dinv2", [128, B])
        enz = sb("enz", [128, B])
        mhalf = sb("mhalf", [128, B])
        stage = sb("stage", [128, 2, 4, 128])
        ie = sb("ie", [128, 4, 128])
        zc = sb("zc", [128, 8])
        okc = sb("okc", [128, OCTETS])
        okz = sb("okz", [128, 10])
        flagc = sb("flagc", [128, 8])
        flag = sb("flag", [1, 1], i32)
        onec = sb("onec", [128, 1])
        nl2 = sb("nl2", [128, 1])

        def small(buf, k, n=1):
            piece = buf[:, 512 * k:512 * (k + n)]
            return piece.rearrange("p (n b c) -> p n b c", n=n, b=GR) if n > 1 else \
                piece.rearrange("p (b c) -> p b c", b=GR)

        ef, hf, yf = (w[:, :, :].rearrange("p k m -> p (k m)") for w in (e, h, y))
        x1s = small(hf, 0, 2)
        x1t = hf[:, 1024:2048].rearrange("p (k b i) -> p k b i", k=2, b=GR // 2)
        b2s, xb = small(yf, 0, 2), small(yf, 2, 2)
        u1 = small(ef, 0, 2)
        xc1, xc2 = small(ef, 2), small(ef, 3)
        sq1, sq2 = small(t, 0), small(t, 1)
        v, b1s = small(junk, 0), small(junk, 1)
        stf = stage[:, :, :, :].rearrange("p k g i -> p (k g i)")
        half, v2 = small(stf, 0), small(stf, 1)
        Y = SRT[:, :, :].rearrange("p a n -> p (a n)")[:, 0:2 * 4 * GR * F]\
            .rearrange("p (k w b c) -> p k w b c", k=2, w=4, b=GR)
        sm = sb("sm", [128, 2, GR])
        vs = sb("vs", [128, 2, GR])
        rs = sb("rs", [128, 2, GR])

        E = ce[:, :].bitcast(bf16).rearrange("p (c u m) -> p c u m", c=KCH, u=UB)
        kbias = cf[:, 0:1]
        ident = cf[:, 1:129]
        fold2 = cf[:, 129:193]
        ncap = cf[:, 193:321]
        e0, t0, h0, tq, phi0 = (cols[:, n:n + 1] for n in range(5))
        adj_o = adj.rearrange("b (o r i) j -> b o r i j", r=OCT, i=2)
        VG = PR[:, 0:OCT, :]
        LNP = V[:, :, :].rearrange("p a n -> p (a n)").rearrange("p (b i) -> p b i", b=B)

        Z0 = pb("Z0", [128, UC])
        Z1 = pb("Z1", [128, UC])
        Z2 = pb("Z2", [128, UC])
        PTPf = pb("PTPf", [128, 512])
        PTP = PTPf[:, :].bitcast(bf16)
        PM = pb("PM", [128, 512])

        QF = Z0[:, :].rearrange("p (b a c) -> p b a c", b=GR, a=2)
        QT = Z1[:, 0:512].rearrange("p (b i) -> p b i", b=GR // 2)
        QY = [Z1[:, 512:1024], Z2[:, 0:512]]
        Q2 = Z2[:, 512:1024].rearrange("p (b c) -> p b c", b=GR)
        Q1 = PTPf[:, :].rearrange("p (b c) -> p b c", b=GR)
        QO = PM[:, :].rearrange("p (b c) -> p b c", b=GR)

        names = """s_adjv s_adjn s_x s_cst s_w s_zero s_ones s_ident s_setA s_setP s_setD
                   s_arg s_e s_z1 s_t s_h s_z2 s_y s_p s_run s_mx s_mr s_sorted s_gath s_split
                   s_gp s_ptt s_pt s_deg s_d s_stage s_ltt s_ltev s_lt s_chk s_flp s_fl
                   s_lnp s_fold s_v s_ln s_x1 s_xt s_xte s_b3 s_b3e s_b2 s_b2e s_b1 s_b1e s_o s_fin s_out
                   s_rs s_gx s_ch s_gch s_hf s_u1 s_u1b s_xbp s_sq1 s_sq2 s_vs1 s_vs2 s_rs1 s_rs2 s_xc1 s_xc2 s_y4 s_ye s_l2 s_l1 s_l0 s_b2v s_b1v s_sf s_rdy s_wl s_dz g_load g_d g_split g_tr g_pt g_arg g_e g_z g_zb g_sp g_ab g_t g_l g_h g_acc g_ch g_parts s_parts g_done
                   s_vs s_b3h s_xb s_op""".split()
        S = {n: sem(n) for n in names}
        s_adjv = [sem(f"s_adjv{k}") for k in range(OCTETS)]
        s_adjn = [sem(f"s_adjn{k}") for k in range(8)]

        block = ctx.enter_context(nc.Block())

        @block.sync
        def _(sp):
            def rows(n):
                for i2 in range(2):
                    src = adj_o[:, ORDER[n], :, i2, :]
                    sp.dma_start(V[64 * i2:64 * i2 + 64, OCT * ORDER[n]:OCT * ORDER[n] + OCT, :], src)\
                        .then_inc(s_adjv[n], 16)

            rows(0)
            sp.dma_start(cf[:, :], c_f).then_inc(S["s_cst"], 16)
            sp.dma_start(ce[0:KROWS, 0:UB * 128], c_e[:, 0:UB * 128]).then_inc(S["s_cst"], 16)
            sp.wait_ge(S["s_zero"], 1)
            for a in range(2):
                sp.dma_start(w1bd[64 * a:64 * a + 64, 0, 64 * a:64 * a + 64], W1[0:64, :]).then_inc(S["s_w"], 16)
                sp.dma_start(w2bd[64 * a:64 * a + 64, 64 * a:64 * a + 64], W2).then_inc(S["s_w"], 16)
                sp.dma_start(b1c[64 * a:64 * a + 64, :], b1.rearrange("(f a) -> f a", a=1)).then_inc(S["s_w"], 16)
                sp.dma_start(b2c[64 * a:64 * a + 64, :], b2.rearrange("(f a) -> f a", a=1)).then_inc(S["s_w"], 16)
            for n in range(1, OCTETS):
                rows(n)
            for g in range(8):
                sp.dma_start(LT[:, 8 * g:8 * g + 8, :], adj[8 * g:8 * g + 8, :, :].rearrange("b i j -> i b j"))\
                    .then_inc(s_adjn[g], 16)
            sp.dma_start(X[:, :, :], x.rearrange("b i c -> i b c")).then_inc(S["s_x"], 16)
            for a in range(2):
                sp.dma_start(wl[64 * a:64 * a + 64, :, 64 * a:64 * a + 64], WL.rearrange("k a c o -> (a c) k o"))\
                    .then_inc(S["s_wl"], 16)
                for c in range(1, KCH):
                    k = min(64, NRBF - 64 * c)
                    sp.dma_start(w1bd[64 * a:64 * a + k, c, 64 * a:64 * a + 64], W1[64 * c:64 * c + k, :])\
                        .then_inc(S["s_wl"], 16)
            sp.dma_start(biasr[:, :], biasL.rearrange("a b o -> (a b) o").broadcast_to([128, F]))\
                .then_inc(S["s_wl"], 16)
            sp.dma_start(ce[0:KROWS, UB * 128:], c_e[:, UB * 128:]).then_inc(S["s_wl"], 16)
            sp.wait_ge(S["s_fl"], 1)
            general = sp.value_load(flag[0:1, 0:1])
            with sp.If(general != 0):
                with sp.Fori(0, OCTETS) as o:
                    sp.wait_ge(S["g_acc"], GSTEPS * GBLK * o + 1)
                    for i2 in range(2):
                        sp.dma_start(VG[64 * i2:64 * i2 + 64, :, :], adj_o[:, o, :, i2, :])\
                            .then_inc(S["g_load"], 16)
            for g in range(8):
                sp.wait_ge(S["s_fin"], g + 1)
                sp.dma_start(out[8 * g:8 * g + 8, :, :].rearrange("b i c -> i b c"), X[:, 8 * g:8 * g + 8, :])\
                    .then_inc(S["s_out"], 16)
            sp.wait_ge(S["s_out"], 8 * 16)

        @block.scalar
        def _(act):
            act.preload_act_table_set("natural_log_exp_and_others")
            act.wait_ge(S["s_cst"], 32)
            act.wait_ge(S["s_w"], 8 * 16)
            nc.scalar.activation(e0, kbias, ACT.Exp).then_inc(S["s_setA"], 1)
            act.wait_ge(S["s_setP"], 3)
            nc.scalar.activation(t0, PM[:, 2:3], ACT.Exp, bias=b1c[:, :]).then_inc(S["s_setA"], 1)
            act.wait_ge(S["s_setA"], 2)
            nc.scalar.activation(h0, t0, ACT.Ln, bias=1.0).then_inc(S["s_setA"], 1)
            act.wait_ge(S["s_setP"], 4)
            act.wait_ge(S["s_setD"], 3)
            nc.scalar.activation(tq, PM[:, 3:4], ACT.Exp, bias=b2p[:, :]).then_inc(S["s_setA"], 1)
            act.wait_ge(S["s_setA"], 4)
            nc.scalar.activation(phi0, tq, ACT.Ln, bias=1.0).then_inc(S["s_setA"], 1)

            def exp_rbf(q, k):
                act.wait_ge(S["s_arg"], q + 1)
                nc.scalar.activation(e[:, k, :], Z0[:, :], ACT.Exp).then_inc(S["s_e"], 1)

            def exp_z1(q, k):
                act.wait_ge(S["s_z1"], q + 1)
                act.wait_ge(S["s_h"], q) if not isinstance(q, int) or q else None
                nc.scalar.activation(t[:, :], Z1[:, :], ACT.Exp, bias=b1c[:, :]).then_inc(S["s_t"], 1)

            def ln_z1(q, k):
                act.wait_ge(S["s_t"], q + 1)
                nc.scalar.activation(h[:, k, :], t[:, :], ACT.Ln, bias=1.0).then_inc(S["s_h"], 1)

            def exp_z2(q, k, wait=True):
                act.wait_ge(S["s_z2"], q + 1)
                if wait:
                    act.wait_ge(S["s_p"], q - 1)
                nc.scalar.activation(y[:, k, :], Z2[:, :], ACT.Exp, bias=b2p[:, :]).then_inc(S["s_y"], 1)

            for q in range(4):
                exp_rbf(q, q % 2)
                if q >= 1:
                    exp_z1(q - 1, (q - 1) % 2)
                if q >= 3:
                    exp_z2(q - 3, (q - 3) % 2, wait=False)
                if q >= 1:
                    ln_z1(q - 1, (q - 1) % 2)
            exp_rbf(4, 0)
            exp_z1(3, 1)
            exp_z2(1, 1, wait=False)
            ln_z1(3, 1)
            exp_rbf(5, 1)
            exp_z1(4, 0)
            exp_z2(2, 0)
            ln_z1(4, 0)
            with act.Fori(3, UNITS // 2) as m:
                for k in range(2):
                    exp_rbf(2 * m + k, k)
                    exp_z1(2 * m + k - 1, 1 - k)
                    exp_z2(2 * m + k - 3, 1 - k)
                    ln_z1(2 * m + k - 1, 1 - k)
            exp_z1(UNITS - 1, 1)
            exp_z2(UNITS - 3, 1)
            ln_z1(UNITS - 1, 1)
            exp_z2(UNITS - 2, 0)
            exp_z2(UNITS - 1, 1)

            def logs(g):
                nc.scalar.activation(LNP[:, GR * g:GR * g + GR, :].rearrange("p b i -> p i b"),
                                     PR[:, :, :].rearrange("p t (i b) -> p (t i) b", i=2)[:, :, GR * g:GR * g + GR],
                                     ACT.Ln).then_inc(S["s_lnp"], 1)

            act.wait_ge(S["s_p"], UNITS)
            for g in range(8):
                logs(g)

            act.wait_ge(S["s_fl"], 1)
            general = act.value_load(flag[0:1, 0:1])
            with act.If(general != 0):
                with act.Fori(0, OCTETS * GBLK * GSTEPS) as m:
                    for c in range(KCH):
                        act.wait_ge(S["g_arg"], KCH * m + c + 1)
                        nc.scalar.activation(e[:, 0, :], Z0[:, :], ACT.Exp).then_inc(S["g_e"], 1)
                    for layer in range(2):
                        act.wait_ge(S["g_ab"], 2 * m + layer + 1)
                        nc.scalar.activation(t[:, :], y[:, 0, :], ACT.Exp, scale=-1.0).then_inc(S["g_t"], 1)
                        act.wait_ge(S["g_t"], 2 * m + layer + 1)
                        nc.scalar.activation(h[:, 1, :], t[:, :], ACT.Ln, bias=1.0).then_inc(S["g_l"], 1)
                act.wait_ge(S["g_done"], 1)

            act.wait_ge(S["s_fl"], 1)

            def first_half(g):
                act.wait_ge(S["s_fold"], g + 1)
                if g >= 1:
                    act.wait_ge(S["s_sf"], g)
                nc.scalar.activation(half, QF[:, :, 0, :], ACT.Copy).then_inc(S["s_hf"], 1)

            def square1(g):
                act.wait_ge(S["s_xc1"], g + 1)
                nc.scalar.activation(sq1, xc1, ACT.Square).then_inc(S["s_sq1"], 1)

            first_half(0)
            square1(0)
            for g in range(10):
                k = g % 2
                if g < 8:
                    act.wait_ge(S["s_xt"], g + 1)
                    nc.scalar.activation(x1t[:, k, :, :], QT, ACT.Copy).then_inc(S["s_xte"], 1)
                if g + 1 < 8:
                    first_half(g + 1)
                    square1(g + 1)
                if g < 8:
                    if g >= 2:
                        act.wait_ge(S["s_xbp"], g - 1)
                        act.wait_ge(S["s_b2v"], g - 1)
                    for b in range(GR // 2):
                        act.wait_ge(S["s_y4"], GR // 2 * g + b + 1)
                        nc.scalar.activation(Y[:, k, :, 2 * b:2 * b + 2, :],
                                             QY[b % 2].rearrange("p (w b c) -> p w b c", w=4, b=2), ACT.Copy)\
                            .then_inc(S["s_ye"], 1)
                if 1 <= g < 9:
                    act.wait_ge(S["s_xc2"], g)
                    nc.scalar.activation(sq2, xc2, ACT.Square).then_inc(S["s_sq2"], 1)

        @block.tensor
        def _(pe):
            def mm(o, w, r, start=True, stop=True):
                return nc.tensor.matmul(o, w, r, start=start, stop=stop)

            def setup():
                pe.wait_ge(S["s_w"], 8 * 16)
                pe.wait_ge(S["s_setD"], 2)
                mm(PM[:, 0:1], w2bd[:, :], nl2[:, :]).then_inc(S["s_setP"], 1)
                mm(PM[:, 1:2], w1abs[:, :], onec[:, :]).then_inc(S["s_setP"], 1)
                pe.wait_ge(S["s_setA"], 1)
                pe.wait_ge(S["s_setD"], 4)
                mm(PM[:, 2:3], w1bd[:, 0, :], e0).then_inc(S["s_setP"], 1)
                pe.wait_ge(S["s_setA"], 3)
                mm(PM[:, 3:4], w2bd[:, :], h0).then_inc(S["s_setP"], 1)
                pe.wait_ge(S["s_setD"], 5)
                mm(PM[:, 64:128], ncap[0:64, :], diag[:, :]).then_inc(S["s_setP"], 1)

            def args(q, u, k, first=False):
                if not first:
                    pe.wait_ge(S["s_e"], q)
                for c in range(2):
                    last = mm(Z0[:, 512 * c:512 * c + 512], E[0:KROWS, 0, u, :],
                              PT[0:KROWS, k, 512 * c:512 * c + 512])
                last.then_inc(S["s_arg"], 1)

            def layer1(q, u):
                pe.wait_ge(S["s_e"], q + 1)
                pe.wait_ge(S["s_t"], q)
                for c in range(2):
                    last = mm(Z1[:, 512 * c:512 * c + 512], w1bd[:, 0, :], e[:, u % 2, 512 * c:512 * c + 512])
                last.then_inc(S["s_z1"], 1)

            def layer2(q, u):
                pe.wait_ge(S["s_h"], q + 1)
                pe.wait_ge(S["s_y"], q)
                for c in range(2):
                    last = mm(Z2[:, 512 * c:512 * c + 512], w2bd[:, :], h[:, u % 2, 512 * c:512 * c + 512])
                last.then_inc(S["s_z2"], 1)

            def transpose_block(bk, k):
                pe.wait_ge(S["s_split"], bk + 1)
                for r in range(OCT):
                    last = nc.tensor.transpose(PTP[0:PROWS, 128 * r:128 * r + 128], BUF[:, k, r, :], identb[:, :])
                last.then_inc(S["s_ptt"], 1)

            def transpose_lap(n, k):
                pe.wait_ge(S["s_stage"], n + 1)
                pe.wait_ge(S["s_ltev"], n)
                for g in range(4):
                    last = nc.tensor.transpose(PM[:, 128 * g:128 * g + 128], stage[:, k, g, :], ident)
                last.then_inc(S["s_ltt"], 1)

            setup()
            pe.wait_ge(S["s_ident"], 2)
            pe.wait_ge(S["s_ones"], 1)
            transpose_block(0, 0)
            pe.wait_ge(S["s_pt"], 1)
            args(0, 0, 0, first=True)

            def block_body(bk, k, first=False, last=False, lap=True):
                for u in range(UB):
                    q = UB * bk + u
                    if lap and u in (3, 7):
                        transpose_lap(2 * (bk - 1) + (u == 7), int(u == 7))
                    if u == 4 and not last:
                        transpose_block(bk + 1, 1 - k)
                    if u < UB - 1:
                        args(q + 1, u + 1, k)
                    elif not last:
                        pe.wait_ge(S["s_pt"], bk + 2)
                        args(q + 1, 0, 1 - k)
                    layer1(q, u)
                    if not (first and u < 2):
                        layer2(q - 2, u)

            block_body(0, 0, first=True, lap=False)
            pe.wait_ge(S["s_setD"], 6)
            for bk in range(1, NBLK):
                block_body(bk, bk % 2, last=bk == NBLK - 1)
            layer2(UNITS - 2, 0)
            layer2(UNITS - 1, 1)

            pe.wait_ge(S["s_chk"], 1)
            mm(PM[0:1, 0:1], flagc[:, 7:8], onec[:, :]).then_inc(S["s_flp"], 1)

            pe.wait_ge(S["s_lnp"], OCTETS)
            pe.wait_ge(S["s_lt"], LTB)
            pe.wait_ge(S["s_wl"], 8 * 16)
            pe.wait_ge(S["s_fl"], 1)
            general = pe.value_load(flag[0:1, 0:1])
            with pe.If(general != 0):
                with pe.Fori(0, OCTETS * GBLK) as n:
                    pe.wait_ge(S["g_split"], n + 1)
                    for r in range(OCT):
                        last = nc.tensor.transpose(PTP[0:PROWS, 128 * r:128 * r + 128], BUF[:, 0, r, :], identb[:, :])
                    last.then_inc(S["g_tr"], 1)
                    pe.wait_ge(S["g_pt"], n + 1)
                    for u in range(GSTEPS):
                        m = GSTEPS * n + u
                        pe.wait_ge(S["g_acc"], m + 1)
                        for c in range(KCH):
                            if c:
                                pe.wait_ge(S["g_e"], KCH * m + c)
                            for a in range(2):
                                last = mm(Z0[:, 512 * a:512 * a + 512], E[0:KROWS, c, u, :],
                                          PT[0:KROWS, 0, 512 * a:512 * a + 512])
                            last.then_inc(S["g_arg"], 1)
                            pe.wait_ge(S["g_e"], KCH * m + c + 1)
                            for a in range(2):
                                last = mm(Z1[:, 512 * a:512 * a + 512], w1bd[:, c, :], e[:, 0, 512 * a:512 * a + 512],
                                          start=c == 0, stop=c == KCH - 1)
                        last.then_inc(S["g_z"], 1)
                        pe.wait_ge(S["g_h"], m + 1)
                        for a in range(2):
                            last = mm(Z2[:, 512 * a:512 * a + 512], w2bd[:, :], h[:, 0, 512 * a:512 * a + 512])
                        last.then_inc(S["g_z"], 1)
                pe.wait_ge(S["g_done"], 1)

            def fold(g):
                if g >= 1:
                    pe.wait_ge(S["s_hf"], g)
                    pe.wait_ge(S["s_sf"], g)
                for b in range(GR):
                    last = nc.tensor.transpose(QF[:, b, :, :].rearrange("p a c -> p (a c)"), LNP[:, GR * g + b, :],
                                               ident)
                last.then_inc(S["s_fold"], 1)

            def laplacian(o, g, what):
                for b in range(GR):
                    last = mm(o[:, b, :], LT[:, GR * g + b, :], what[:, b, :])
                return last

            fold(0)
            for g in range(9):
                k = g % 2
                if g < 8:
                    pe.wait_ge(S["s_x1"], g + 1)
                    for b in range(0, GR, 2):
                        last = nc.tensor.transpose(QT[:, b // 2, :],
                                                   x1s[:, k, b:b + 2, :].rearrange("p b c -> p (b c)"), ident)
                    last.then_inc(S["s_xt"], 1)
                if g + 1 < 8:
                    fold(g + 1)
                if g >= 1:
                    pe.wait_ge(S["s_b2v"], g)
                    laplacian(Q1, g - 1, b2s[:, 1 - k, :, :]).then_inc(S["s_l1"], 1)
                if g < 8:
                    pe.wait_ge(S["s_xte"], g + 1)
                    for b in range(GR // 2):
                        if 4 * g + b >= 2:
                            pe.wait_ge(S["s_ye"], 4 * g + b - 1)
                        mm(QY[b % 2], x1t[:, k, b, :], wl[:, :, :].rearrange("p w m -> p (w m)"))\
                            .then_inc(S["s_y4"], 1)
                if g >= 1:
                    pe.wait_ge(S["s_b1v"], g)
                    laplacian(QO, g - 1, b1s).then_inc(S["s_l0"], 1)
                if g < 8:
                    pe.wait_ge(S["s_ye"], 4 * g + 4)
                    laplacian(Q2, g, Y[:, k, 3, :, :]).then_inc(S["s_l2"], 1)

        @block.vector
        def _(dve):
            V_ = nc.vector
            chain = [0]

            def link(ins):
                chain[0] += 1
                ins.then_inc(S["s_ch"], 1)
                dve.wait_ge(S["s_ch"], chain[0])

            V_.memset(nl2[:, :], -LOG2)
            V_.memset(onec[:, :], 1.0).then_inc(S["s_setD"], 1)

            def sort(first):
                if first % OCT == 0:
                    dve.wait_ge(s_adjv[first // OCT], 32)
                pair = [OCT * ORDER[n // OCT] + n % OCT for n in (first, first + 1)]
                rounds = max(-(-CAPS[a] // 8) for a in pair)
                for k in range(rounds):
                    for a in pair:
                        last = V_.max(SRT[:, a, 8 * k:8 * k + 8], V[:, a, :])
                    if k < rounds - 1:
                        link(last)
                        for a in pair:
                            mr = V_.match_replace(V[:, a, :], SRT[:, a, 8 * k:8 * k + 8], V[:, a, :], 0.0)
                        link(mr)
                last.then_inc(S["s_sorted"], 1)

            for n in range(0, OCT, 2):
                sort(n)
            dve.wait_ge(S["s_cst"], 32)
            V_.tensor_copy(identb[:, :], ident).then_inc(S["s_ident"], 1)
            V_.tensor_scalar(ident2[:, :], ident, 2.0, None, ALU.mult).then_inc(S["s_ident"], 1)
            dve.wait_ge(S["s_w"], 8 * 16)
            V_.scalar_tensor_tensor(w1abs[:, :], w1bd[:, 0, :], -1.0, w1bd[:, 0, :], ALU.mult, ALU.max)\
                .then_inc(S["s_setD"], 1)
            V_.memset(PT[ONES:KROWS, :, :], 1.0).then_inc(S["s_ones"], 1)
            dve.wait_ge(S["s_setP"], 2)
            V_.tensor_tensor(b2p[:, :], PM[:, 0:1], b2c[:, :], ALU.add).then_inc(S["s_setD"], 1)
            link(V_.scalar_tensor_tensor(zc[:, 0:1], b1c[:, :], -1.0, b1c[:, :], ALU.mult, ALU.max))
            V_.tensor_tensor(zc[:, 1:2], PM[:, 1:2], zc[:, 0:1], ALU.add).then_inc(S["s_setD"], 1)
            dve.wait_ge(S["s_setA"], 5)
            V_.tensor_scalar(diag[:, :], ident[0:64, 0:64], phi0[0:64, :], None, ALU.mult).then_inc(S["s_setD"], 1)
            dve.wait_ge(S["s_setP"], 5)
            V_.tensor_scalar(C1[:, :], PM[:, 64:128], 1.0 - N * LOG2, None, ALU.add).then_inc(S["s_setD"], 1)

            def evac_block(bk):
                dve.wait_ge(S["s_ptt"], bk + 1)
                if bk >= 2:
                    dve.wait_ge(S["s_arg"], UB * (bk - 1))
                V_.tensor_copy(PT[0:PROWS, bk % 2, :], PTP[0:PROWS, :]).then_inc(S["s_pt"], 1)

            def evac_lap(n):
                dve.wait_ge(S["s_ltt"], n + 1)
                dve.wait_ge(S["s_d"], 1 + n // 8)
                V_.tensor_tensor(LT[:, 4 * n:4 * n + 4, :], PM[:, :].rearrange("p (g i) -> p g i", g=4),
                                 dinv[:, 4 * n:4 * n + 4].unsqueeze(2).broadcast_to([128, 4, 128]), ALU.mult)\
                    .then_inc(S["s_ltev"], 1)

            counts = [0]

            def after_count():
                if counts[0]:
                    dve.wait_ge(S["s_dz"], counts[0])
                counts[0] += 1

            def kept_checks():
                dve.wait_ge(S["s_gath"], 1)
                for n in range(2):
                    at = NBLK * BI // 2 * n
                    after_count()
                    V_.tensor_scalar(junk[:, 0:NBLK * BI],
                                     D[:, at:at + NBLK * BI // 2, :].rearrange("p f s -> p (f s)"),
                                     0.0, 0.0, ALU.is_equal, ALU.add, accum_out=okz[:, 8 + n:9 + n])\
                        .then_inc(S["s_dz"], 1)
                after_count()
                V_.tensor_reduce(flagc[:, 0:1], D[:, :, :], AX.XY, ALU.max).then_inc(S["s_dz"], 1)

            def products_check(o):
                after_count()
                V_.tensor_scalar(junk[:, :], PR[:, OCT * o:OCT * o + OCT, :].rearrange("p t m -> p (t m)"), PMAX,
                                 0.0, ALU.is_le, ALU.add, accum_out=okc[:, o:o + 1]).then_inc(S["s_dz"], 1)

            evac_block(0)
            for n in range(OCT, SORT_AHEAD, 2):
                sort(n)
            runs_done = 0
            for bk in range(NBLK):
                for u in range(UB):
                    q = UB * bk + u
                    if u == 2 and bk + 1 < NBLK:
                        evac_block(bk + 1)
                    if bk == 0:
                        dve.wait_ge(s_adjn[u], 16)
                        V_.tensor_reduce(deg[:, 8 * u:8 * u + 8], LT[:, 8 * u:8 * u + 8, :], AX.X, ALU.add)\
                            .then_inc(S["s_deg"], 1)
                    if bk == 1:
                        after_count()
                        V_.tensor_scalar(junk[:, :], LT[:, 8 * u:8 * u + 8, :].rearrange("p b j -> p (b j)"), 0.0,
                                         0.0, ALU.is_equal, ALU.add, accum_out=okz[:, u:u + 1]).then_inc(S["s_dz"], 1)
                    if bk >= 1 and u in (2, 6):
                        evac_lap(2 * (bk - 1) + (u == 6))
                    if q == UNITS - 6:
                        kept_checks()
                    if SORT_AHEAD + 2 * q < TILES:
                        sort(SORT_AHEAD + 2 * q)
                    dve.wait_ge(S["s_y"], q + 1)
                    pieces = runs_of_unit(q)
                    for n, (r, live, tile, fresh, o) in enumerate(pieces):
                        src = y[:, q % 2, 128 * r:128 * (r + live)].rearrange("p (t m) -> p t m", m=128)
                        dst = PR[:, tile:tile + live, :]
                        if runs_done:
                            dve.wait_ge(S["s_run"], runs_done)
                        if fresh:
                            ins = V_.tensor_scalar(dst, src, 1.0, None, ALU.add)
                        else:
                            ins = V_.scalar_tensor_tensor(dst, src, 1.0, dst, ALU.add, ALU.mult)
                        ins.then_inc(S["s_run"], 1)
                        runs_done += 1
                    dve.wait_ge(S["s_run"], runs_done)
                    V_.sem_inc(S["s_p"], 1)
                    for n, o in enumerate(ORDER):
                        if OCT * q < OCTET_END[o] <= OCT * q + OCT:
                            products_check(o)

            dve.wait_ge(S["s_dz"], DZ_ALL)
            V_.tensor_reduce(flagc[:, 1:2], okz[:, 0:8], AX.X, ALU.add)
            V_.tensor_reduce(flagc[:, 2:3], okz[:, 8:10], AX.X, ALU.add)
            link(V_.tensor_reduce(zc[:, 2:3], okc[:, :], AX.X, ALU.add))
            link(V_.tensor_tensor(flagc[:, 3:4], flagc[:, 2:3], flagc[:, 1:2], ALU.subtract))
            link(V_.tensor_tensor(flagc[:, 5:6], flagc[:, 3:4], zc[:, 2:3], ALU.subtract))
            link(V_.tensor_scalar(flagc[:, 4:5], flagc[:, 0:1], DMAX, None, ALU.is_le))
            link(V_.scalar_tensor_tensor(flagc[:, 6:7], zc[:, 1:2], ZMAX, flagc[:, 4:5], ALU.is_le, ALU.add))
            link(V_.tensor_tensor(flagc[:, 7:8], flagc[:, 5:6], flagc[:, 6:7], ALU.subtract))
            V_.tensor_scalar(flagc[:, 7:8], flagc[:, 7:8], float(2 + OCTETS * UC + B * N - 2 * NBLK * BI), None,
                             ALU.add).then_inc(S["s_chk"], 1)
            dve.wait_ge(S["s_flp"], 1)
            V_.tensor_copy(flag[:, :], PM[0:1, 0:1]).then_inc(S["s_fl"], 1)

            dve.wait_ge(S["s_fl"], 1)
            general = dve.value_load(flag[0:1, 0:1])
            with dve.If(general != 0):
                dve.wait_ge(S["s_lnp"], OCTETS)
                V_.memset(V[:, :, :], 0.0).then_inc(S["g_acc"], 1)
                with dve.Fori(0, OCTETS) as o:
                    with dve.Fori(0, GBLK) as c:
                        n = GBLK * o + c
                        dve.wait_ge(S["g_load"], 32 * o + 32)
                        rows = VG.rearrange("p r (c u s) -> p c u r s", c=GBLK, u=UB)
                        V_.tensor_copy(D[:, 0:BI, :].rearrange("p (u r) s -> p u r s", u=UB), rows[:, c])\
                            .then_inc(S["g_d"], 1)
                        dve.wait_ge(S["g_tr"], n + 1)
                        V_.tensor_copy(PT[0:PROWS, 0, :], PTP[0:PROWS, :]).then_inc(S["g_pt"], 1)
                        with dve.Fori(0, GSTEPS) as u:
                            m = GSTEPS * n + u
                            for layer, (z, bias) in enumerate(((Z1, b1c), (Z2, b2p))):
                                dve.wait_ge(S["g_z"], 2 * m + layer + 1)
                                V_.tensor_scalar(junk[:, :], z[:, :], bias[:, :], None, ALU.add)\
                                    .then_inc(S["g_zb"], 1)
                                dve.wait_ge(S["g_zb"], 2 * m + layer + 1)
                                V_.scalar_tensor_tensor(y[:, 0, :], junk[:, :], -1.0, junk[:, :], ALU.mult, ALU.max)\
                                    .then_inc(S["g_ab"], 1)
                                dve.wait_ge(S["g_l"], 2 * m + layer + 1)
                                V_.scalar_tensor_tensor(h[:, 0, :], junk[:, :], 0.0, h[:, 1, :], ALU.max, ALU.add)\
                                    .then_inc(S["g_sp"], 1)
                                dve.wait_ge(S["g_sp"], 2 * m + layer + 1)
                                if layer == 0:
                                    dve.sem_inc(S["g_h"], 1)
                            sums = LNP.rearrange("p b (o i) -> p o i b", o=OCTETS)[:, o]
                            dve.wait_ge(S["g_acc"], m + 1)
                            V_.tensor_tensor(sums, sums, h[:, 0, :].rearrange("p (i b) -> p i b", b=B), ALU.add)\
                                .then_inc(S["g_acc"], 1)
                V_.memset(C1[:, :], 1.0 - N * LOG2).then_inc(S["g_done"], 1)
                dve.wait_ge(S["g_done"], 1)

            wide = [128, GR, F]

            def centre(src, dst, k):
                link(V_.tensor_reduce(sm[:, k, :], src, AX.X, ALU.add))
                return V_.scalar_tensor_tensor(dst, sm[:, k, :].unsqueeze(2).broadcast_to(wide), -1.0 / F, src,
                                               ALU.mult, ALU.add)

            def start1(g):
                dve.wait_ge(S["s_u1"], g + 1)
                V_.tensor_tensor(v, QF[:, :, 1, :], v2, ALU.add).then_inc(S["s_sf"], 1)
                dve.wait_ge(S["s_sf"], g + 1)
                link(V_.tensor_tensor(v, v, X[:, GR * g:GR * g + GR, :], ALU.mult))
                if g >= 1:
                    dve.wait_ge(S["s_x1"], g)
                centre(v, xc1, 0).then_inc(S["s_xc1"], 1)

            def end1(g):
                dve.wait_ge(S["s_sq1"], g + 1)
                V_.tensor_reduce(vs[:, 0, :], sq1, AX.X, ALU.add).then_inc(S["s_vs1"], 1)
                dve.wait_ge(S["s_rs1"], g + 1)
                if g >= 2:
                    dve.wait_ge(S["s_xbp"], g - 1)
                V_.tensor_tensor(x1s[:, g % 2, :, :], xc1, rs[:, 0, :].unsqueeze(2).broadcast_to(wide), ALU.mult)\
                    .then_inc(S["s_x1"], 1)

            dve.wait_ge(S["s_x"], 16)
            start1(0)
            end1(0)
            for g in range(10):
                k = g % 2
                if 1 <= g < 9:
                    dve.wait_ge(S["s_l2"], g)
                    if g >= 3:
                        dve.wait_ge(S["s_xb"], g - 2)
                    V_.tensor_tensor(b2s[:, 1 - k, :, :], Q2, Y[:, 1 - k, 2, :, :], ALU.add).then_inc(S["s_b2v"], 1)
                if g >= 2:
                    dve.wait_ge(S["s_sq2"], g - 1)
                    V_.tensor_reduce(vs[:, 1, :], sq2, AX.X, ALU.add).then_inc(S["s_vs2"], 1)
                if 1 <= g < 9:
                    dve.wait_ge(S["s_l1"], g)
                    dve.wait_ge(S["s_u1b"], g)
                    V_.tensor_tensor(b1s, Q1, u1[:, 1 - k, :, :], ALU.add).then_inc(S["s_b1v"], 1)
                if g + 1 < 8:
                    start1(g + 1)
                if g >= 2:
                    dve.wait_ge(S["s_rs2"], g - 1)
                    V_.tensor_tensor(X[:, GR * (g - 2):GR * (g - 1), :], xc2,
                                     rs[:, 1, :].unsqueeze(2).broadcast_to(wide), ALU.mult).then_inc(S["s_fin"], 1)
                if g + 1 < 8:
                    end1(g + 1)
                if 1 <= g < 9:
                    dve.wait_ge(S["s_l0"], g)
                    dve.wait_ge(S["s_xb"], g)
                    link(V_.scalar_tensor_tensor(v, QO, 0.5, xb[:, 1 - k, :, :], ALU.mult, ALU.add))
                    if g >= 2:
                        dve.wait_ge(S["s_fin"], g - 1)
                    centre(v, xc2, 1).then_inc(S["s_xc2"], 1)

        @block.gpsimd
        def _(pool):
            G = nc.gpsimd
            G.memset(w1bd[:, :, :], 0.0)
            G.memset(w2bd[:, :], 0.0)
            G.memset(wl[:, :, :], 0.0)
            G.memset(mhalf[:, :], -0.5).then_inc(S["s_zero"], 1)
            chain = [0]

            def link(ins):
                chain[0] += 1
                ins.then_inc(S["s_gch"], 1)
                pool.wait_ge(S["s_gch"], chain[0])

            def gather(bk):
                for o, lev, live, at in LEVELS:
                    if BI * bk <= at < BI * bk + BI:
                        pool.wait_ge(S["s_sorted"], OCT // 2 * (ORDER.index(o) + 1))
                        last = G.tensor_copy(D[:, at:at + live, :],
                                             SRT[:, OCT * o:OCT * o + live, 2 * lev:2 * lev + 2])
                return last

            def block_views(k, first):
                shape = "p (u r) s -> p u r s"
                return (BUF[:, k, :, :].rearrange("p r (u a s) -> p a u r s", u=UB, a=PARTS),
                        D[:, first:first + BI, :].rearrange(shape, u=UB), dd[:, :, :].rearrange(shape, u=UB),
                        r1[:, :, :].rearrange(shape, u=UB), dl[:, :, :].rearrange(shape, u=UB))

            def first_parts(part, dist, square, rest, rest2):
                G.tensor_tensor(square, dist, dist, ALU.mult)
                G.tensor_copy(part[:, 0], dist)
                return G.tensor_tensor(part[:, 3], dist, dist, ALU.mult)

            def second_parts(part, dist, square, rest, rest2):
                G.tensor_tensor(rest, dist, part[:, 0], ALU.subtract)
                G.tensor_tensor(part[:, 1], dist, part[:, 0], ALU.subtract)
                G.tensor_tensor(rest2, square, part[:, 3], ALU.subtract)
                return G.tensor_tensor(part[:, 4], square, part[:, 3], ALU.subtract)

            def third_parts(part, dist, square, rest, rest2):
                G.tensor_tensor(part[:, 2], rest, part[:, 1], ALU.subtract)
                return G.tensor_tensor(part[:, 5], rest2, part[:, 4], ALU.subtract)

            def split(bk):
                if bk >= 2:
                    pool.wait_ge(S["s_ptt"], bk - 1)
                if bk:
                    pool.wait_ge(S["s_split"], bk)
                views = block_views(bk % 2, BI * bk)
                first_parts(*views).then_inc(S["s_parts"], 1)
                pool.wait_ge(S["s_parts"], 2 * bk + 1)
                second_parts(*views).then_inc(S["s_parts"], 1)
                pool.wait_ge(S["s_parts"], 2 * bk + 2)
                third_parts(*views).then_inc(S["s_split"], 1)

            def scale_rows(n):
                if n >= 2:
                    pool.wait_ge(S["s_ltt"], n - 1)
                G.tensor_tensor(stage[:, n % 2, :, :], LT[:, 4 * n:4 * n + 4, :],
                                dinv2[:, 4 * n:4 * n + 4].unsqueeze(2).broadcast_to([128, 4, 128]), ALU.mult)\
                    .then_inc(S["s_stage"], 1)

            def add_diagonal(n):
                if n:
                    pool.wait_ge(S["s_lt"], n)
                link(G.tensor_tensor(ie[:, :, :], ident2[:, :].unsqueeze(1).broadcast_to([128, 4, 128]),
                                     enz[:, 4 * n:4 * n + 4].unsqueeze(2).broadcast_to([128, 4, 128]), ALU.mult))
                pool.wait_ge(S["s_ltev"], n + 1)
                G.tensor_tensor(LT[:, 4 * n:4 * n + 4, :], LT[:, 4 * n:4 * n + 4, :], ie[:, :, :], ALU.add)\
                    .then_inc(S["s_lt"], 1)

            def degree_roots(n):
                pool.wait_ge(S["s_deg"], 4 * n + 4)
                c = slice(32 * n, 32 * n + 32)
                G.tensor_scalar(enz[:, c], deg[:, c], 0.0, None, ALU.is_equal)
                G.tensor_scalar(dinv2[:, c], deg[:, c], 0.0, None, ALU.is_gt)
                link(G.tensor_scalar(dinv[:, c], deg[:, c], 1.2e-38, None, ALU.max))
                link(G.tensor_tensor(dinv[:, c], dinv[:, c], mhalf[:, c], ALU.pow))
                link(G.tensor_scalar(enz[:, c], enz[:, c], -1.0, 1.0, ALU.mult, ALU.add))
                link(G.tensor_tensor(dinv[:, c], dinv[:, c], dinv2[:, c], ALU.mult))
                G.tensor_scalar(dinv2[:, c], dinv[:, c], -2.0, None, ALU.mult).then_inc(S["s_d"], 1)
                pool.wait_ge(S["s_d"], n + 1)

            link(gather(0))
            split(0)
            link(gather(1))
            split(1)
            pool.wait_ge(S["s_ident"], 2)
            degree_roots(0)
            link(gather(2))
            split(2)
            scale_rows(0)
            scale_rows(1)
            degree_roots(1)
            for bk in range(2, NBLK + 2):
                if bk + 1 < NBLK:
                    link(gather(bk + 1))
                    if bk + 1 == NBLK - 1:
                        G.sem_inc(S["s_gath"], 1)
                    split(bk + 1)
                if bk < NBLK:
                    scale_rows(2 * bk - 2)
                    scale_rows(2 * bk - 1)
                if 2 * bk - 3 < LTB:
                    add_diagonal(2 * bk - 4)
                    add_diagonal(2 * bk - 3)

            pool.wait_ge(S["s_fl"], 1)
            general = pool.value_load(flag[0:1, 0:1])
            with pool.If(general != 0):
                with pool.Fori(0, OCTETS * GBLK) as n:
                    pool.wait_ge(S["g_d"], n + 1)
                    views = block_views(0, 0)
                    first_parts(*views).then_inc(S["g_parts"], 1)
                    pool.wait_ge(S["g_parts"], 2 * n + 1)
                    second_parts(*views).then_inc(S["g_parts"], 1)
                    pool.wait_ge(S["g_parts"], 2 * n + 2)
                    third_parts(*views).then_inc(S["g_split"], 1)
                pool.wait_ge(S["g_done"], 1)

            def root(n, k, ready, done):
                pool.wait_ge(ready, n)
                link(G.tensor_scalar(rs[:, k, :], vs[:, k, :], 1.0 / F, EPS, ALU.mult, ALU.add))
                G.tensor_tensor(rs[:, k, :], rs[:, k, :], mhalf[:, 0:GR], ALU.pow).then_inc(done, 1)

            def half_sums(g):
                pool.wait_ge(S["s_hf"], g + 1)
                if g >= 1:
                    pool.wait_ge(S["s_sf"], g)
                G.tensor_tensor(v2, half, C1[:, :].unsqueeze(1).broadcast_to([128, GR, F]), ALU.add)\
                    .then_inc(S["s_u1"], 1)

            half_sums(0)
            root(1, 0, S["s_vs1"], S["s_rs1"])
            for g in range(10):
                k = g % 2
                if 1 <= g < 9:
                    pool.wait_ge(S["s_b2v"], g)
                    G.tensor_tensor(xb[:, 1 - k, :, :], xb[:, 1 - k, :, :], b2s[:, 1 - k, :, :], ALU.subtract)\
                        .then_inc(S["s_xb"], 1)
                if g >= 2:
                    root(g - 1, 1, S["s_vs2"], S["s_rs2"])
                if g + 1 < 8:
                    half_sums(g + 1)
                    root(g + 2, 0, S["s_vs1"], S["s_rs1"])
                if g < 8:
                    pool.wait_ge(S["s_ye"], 4 * g + 4)
                    if g >= 2:
                        pool.wait_ge(S["s_xc2"], g - 1)
                    G.tensor_tensor(u1[:, k, :, :], Y[:, k, 1, :, :], Y[:, k, 3, :, :], ALU.subtract)\
                        .then_inc(S["s_u1b"], 1)
                    link(G.tensor_tensor(xb[:, k, :, :], Y[:, k, 0, :, :], x1s[:, k, :, :], ALU.add))
                    G.tensor_tensor(xb[:, k, :, :], xb[:, k, :, :],
                                    biasr[:, :].unsqueeze(1).broadcast_to([128, GR, F]), ALU.add)\
                        .then_inc(S["s_xbp"], 1)
                    pool.wait_ge(S["s_xbp"], g + 1)


def _bf16_bits(a):
    b = np.ascontiguousarray(a, np.float32).view(np.uint32).astype(np.uint64)
    return ((b + 0x7fff + ((b >> 16) & 1)) >> 16).astype(np.uint16)


def _constants():
    ce = np.zeros((KROWS, KCH, UB, 2, 64), np.float32)
    k = np.arange(64 * KCH).reshape(KCH, 64)
    for u in range(UB):
        for s in range(2):
            for a in range(PARTS):
                ce[(u * PARTS + a) * 2 + s, :, u, s, :] = 2 * k if a < 3 else -10.0
    rest = np.broadcast_to((-0.1 * k.astype(np.float64) ** 2)[:, None, None, :], (KCH, UB, 2, 64))
    bits = _bf16_bits(ce)
    for n in range(3):
        bits[ONES + n] = _bf16_bits(rest)
        rest = rest - (bits[ONES + n].astype(np.uint32) << 16).view(np.float32)
    cf = np.zeros((128, 1 + 128 + 64 + 128), np.float32)
    cf[:, 0] = -0.1 * (np.arange(128) % 64).astype(np.float64) ** 2
    cf[:, 1:129] = np.eye(128)
    cf[:, 129:193] = np.concatenate([np.eye(64), np.eye(64)])
    cf[:, 193:321] = N - np.repeat(np.array(CAPS), 2)
    return bits.reshape(KROWS, -1), cf


def kernel(x, adj, L0_gnn_W1, L0_gnn_b1, L0_gnn_W2, L0_gnn_b2, L1_gnn_weight, L1_gnn_bias):
    import concourse.bacc as bacc
    from concourse.bass_utils import run_bass_kernel_spmd

    nc = bacc.Bacc("TRN2", target_bir_lowering=False, num_devices=1)
    c_e, c_f = _constants()
    arrays, args = {}, []
    for name, a in (("x", x), ("adj", adj), ("W1", L0_gnn_W1), ("b1", L0_gnn_b1), ("W2", L0_gnn_W2),
                    ("b2", L0_gnn_b2), ("WL", L1_gnn_weight), ("biasL", L1_gnn_bias), ("c_e", c_e), ("c_f", c_f)):
        a = np.ascontiguousarray(a)
        arrays[f"in_{name}"] = a
        args.append(nc.dram_tensor(f"in_{name}", a.shape, mybir.dt.from_np(a.dtype), kind="ExternalInput").ap())
    out = nc.dram_tensor("out_y", (B, N, F), mybir.dt.float32, kind="ExternalOutput").ap()
    build(nc, *args, out)
    r = run_bass_kernel_spmd(nc, [arrays], core_ids=[0])
    return r.results[0]["out_y"]
```

```python
import numpy as np
import concourse.bass as bass
from concourse import mybir
from contextlib import ExitStack

B, N, F = 64, 128, 64
NRBF = 150
LOG2 = float(np.log(2.0))
EPS = 1e-5

TILES = N // 2
OCT = 8
OCTETS = TILES // OCT
CAPS = [56, 38, 34, 30, 28, 26, 24, 24, 24, 22, 22, 22, 20, 20, 20, 18,
        20, 18, 18, 18, 18, 18, 16, 16, 18, 18, 16, 16, 16, 16, 16, 16,
        16, 16, 16, 14, 14, 14, 14, 14, 14, 14, 14, 14, 14, 14, 14, 14,
        14, 14, 14, 14, 14, 14, 14, 12, 14, 14, 14, 14, 14, 14, 14, 12]
GROUPS = B // 8
SLOTMAX = 64

ORDER = [3, 2, 4, 5, 6, 7, 1, 0]
LEVELS = []
ITEMS = 0
assert ORDER[-1] == 0
EARLY = 4
for o, first, behind in [(o, 0, EARLY) for o in ORDER[:2]] + [(o, EARLY * (o in ORDER[:2]), SLOTMAX) for o in ORDER]:
    caps = CAPS[OCT * o:OCT * o + OCT]
    levels = list(range(first, min(behind, caps[0] // 2)))
    if o == ORDER[-1]:
        levels = levels[:1] + levels[:0:-1]
    for lev in levels:
        live = sum(c > 2 * lev for c in caps)
        LEVELS.append((o, lev, live, ITEMS))
        ITEMS += live
UB = 8
BI = UB * OCT
NBLK = -(-ITEMS // BI)
assert ITEMS == NBLK * BI
UNITS = NBLK * UB
UC = OCT * 128
SORT_ROUNDS = [(n, k) for n in range(0, TILES, 2) for k in range(-(-CAPS[OCT * ORDER[n // OCT] + n % OCT] // 8))]
SORT_ROUNDS.sort(key=lambda step: (step[0] >= 2 * OCT, step[0] < 2 * OCT and step[1] > 0))
FIRST_ROUNDS = OCT
TWO_OCTETS = sum(n < 2 * OCT for n, _ in SORT_ROUNDS)

PARTS = 6
PROWS = UB * 2 * PARTS
ONES = 96
KROWS = ONES + 3
KCH = 3
DMAX = 3.0
ZMAX = 40.0
PMAX = 2.0 ** 60
GBLK = N // (2 * UB)
GSTEPS = UB
LTB = 16
GR = 8
PIECES = [(g, 0, GR) for g in range(B // GR - 1)] + [(B // GR - 1, 0, GR // 2), (B // GR - 1, GR // 2, GR)]


OCTET_END = {o: max(at + live for p, _, live, at in LEVELS if p == o) for o in ORDER}
DZ_ALL = 8 + 3 + OCTETS


def runs_of_unit(q):
    out = []
    for o, lev, live, at in LEVELS:
        a, b = max(at, OCT * q), min(at + live, OCT * q + OCT)
        if a < b:
            out.append((a - OCT * q, b - a, OCT * o + a - at, lev == 0, o))
    return out


def build(nc, x, adj, W1, b1, W2, b2, WL, biasL, c_e, c_f, out):
    f32, bf16, i32 = mybir.dt.float32, mybir.dt.bfloat16, mybir.dt.int32
    ALU = mybir.AluOpType
    ACT = mybir.ActivationFunctionType
    AX = mybir.AxisListType
    ctx = ExitStack()
    with ctx:
        def sb(name, shape, dt=f32):
            return ctx.enter_context(nc.sbuf_tensor(name, shape, dt))

        def pb(name, shape, dt=f32):
            return ctx.enter_context(nc.psum_tensor(name, shape, dt))

        def sem(name):
            return ctx.enter_context(nc.semaphore(name))

        V = sb("V", [128, TILES, N])
        LT = sb("LT", [128, B, N])
        PR = sb("PR", [128, TILES, 128])
        X = sb("X", [128, B, F])
        SRT = sb("SRT", [128, TILES, SLOTMAX])
        D = sb("D", [128, NBLK * BI, 2])
        BUF = sb("BUF", [128, 2, OCT, UB * 2 * PARTS], bf16)
        PT = sb("PT", [128, 2, UC], bf16)
        r1 = sb("r1", [128, BI, 2])
        dd = sb("dd", [128, BI, 2])
        dl = sb("dl", [128, BI, 2])
        e = sb("e", [128, 2, UC])
        t = sb("t", [128, UC])
        h = sb("h", [128, 2, UC])
        y = sb("y", [128, 2, UC])
        junk = sb("junk", [128, UC])
        ce = sb("ce", [128, KCH * UB * 128], mybir.dt.uint16)
        cf = sb("cf", [128, 1 + 128 + 128])
        identb = sb("identb", [128, 128], bf16)
        ident2 = sb("ident2", [128, 128])
        w1bd = sb("w1bd", [128, KCH, 128])
        w2bd = sb("w2bd", [128, 128])
        w1abs = sb("w1abs", [128, 128])
        b1c = sb("b1c", [128, 1])
        b2c = sb("b2c", [128, 1])
        b2p = sb("b2p", [128, 1])
        wl = sb("wl", [128, 4, 2 * F])
        biasr = sb("biasr", [128, F])
        cols = sb("cols", [128, 8])
        diag = sb("diag", [64, 64])
        C1 = sb("C1", [128, F])
        deg = sb("deg", [128, B])
        dinv = sb("dinv", [128, B])
        dinv2 = sb("dinv2", [128, B])
        enz = sb("enz", [128, B])
        mhalf = sb("mhalf", [128, B])
        stage = sb("stage", [128, 2, 4, 128])
        ie = sb("ie", [128, 4, 128])
        zc = sb("zc", [128, 8])
        okc = sb("okc", [128, OCTETS])
        okz = sb("okz", [128, 10])
        flagc = sb("flagc", [128, 8])
        flag = sb("flag", [1, 1], i32)
        onec = sb("onec", [128, 1])
        epsc = sb("epsc", [128, 1])
        blank = sb("blank", [128, 512], bf16)
        nl2 = sb("nl2", [128, 1])

        def small(buf, k, n=1):
            piece = buf[:, 512 * k:512 * (k + n)]
            return piece.rearrange("p (n b c) -> p n b c", n=n, b=GR) if n > 1 else \
                piece.rearrange("p (b c) -> p b c", b=GR)

        ef, hf, yf = (w[:, :, :].rearrange("p k m -> p (k m)") for w in (e, h, y))
        x1s = small(hf, 0, 2)
        x1t = hf[:, 1024:2048].rearrange("p (k b i) -> p k b i", k=2, b=GR // 2)
        b2s, xb = small(yf, 0, 2), small(yf, 2, 2)
        b3s = small(ef, 0, 2)
        xc1, xc2 = small(ef, 2), small(ef, 3)
        sq1, sq2 = small(t, 0), small(t, 1)
        v, b1s = small(junk, 0), small(junk, 1)
        v3 = PR[:, 0:4, :].rearrange("p k n -> p (k n)").rearrange("p (b c) -> p b c", b=GR)
        stf = stage[:, :, :, :].rearrange("p k g i -> p (k g i)")
        half, v2 = small(stf, 0), small(stf, 1)
        sm = sb("sm", [128, 2, GR])
        vs = sb("vs", [128, 2, GR])
        lnv = sb("lnv", [128, 2, GR])
        rs = sb("rs", [128, 2, GR])

        E = ce[:, :].bitcast(bf16).rearrange("p (c u m) -> p c u m", c=KCH, u=UB)
        kbias = cf[:, 0:1]
        ident = cf[:, 1:129]
        ncap = cf[:, 129:257]
        e0, t0, h0, tq, phi0 = (cols[:, n:n + 1] for n in range(5))
        adj_o = adj.rearrange("b (o r i) j -> b o r i j", r=OCT, i=2)
        VG = PR[:, 0:OCT, :]
        LNP = V[:, :, :].rearrange("p a n -> p (a n)").rearrange("p (b i) -> p b i", b=B)

        Z0 = pb("Z0", [128, UC])
        Z1 = pb("Z1", [128, UC])
        Z2 = pb("Z2", [128, UC])
        PTPf = pb("PTPf", [128, 512])
        PTP = PTPf[:, :].bitcast(bf16)
        PM = pb("PM", [128, 512])

        QF = Z0[:, :].rearrange("p (b a c) -> p b a c", b=GR, a=2)
        QT = Z1[:, 0:512].rearrange("p (b i) -> p b i", b=GR // 2)
        Q3 = Z1[:, 512:1024].rearrange("p (b c) -> p b c", b=GR)
        Q2 = Z2[:, 0:512].rearrange("p (b c) -> p b c", b=GR)
        Q1 = Z2[:, 512:1024].rearrange("p (b c) -> p b c", b=GR)
        QO = PM[:, :].rearrange("p (b c) -> p b c", b=GR)

        names = """s_blank s_lv1 s_lv2 s_x s_cst s_w s_zero s_ones s_ident s_setA s_setP s_setD s_arg s_e
                   s_z1 s_t s_h s_z2 s_y s_p s_run s_mx s_gath s_split s_ptt s_pt s_deg s_d s_stage s_ltt
                   s_ltev s_lt s_chk s_flp s_fl s_lnp s_fold s_x1 s_xt s_xte s_o s_fin s_out s_ch s_gch s_hf
                   s_u1 s_xbp s_sq1 s_sq2 s_vs1 s_vs2 s_rs1 s_rs2 s_xc1 s_xc2 s_q3 s_b3c s_b2c s_wl2 s_l2
                   s_l1 s_l0 s_b1v s_sf s_wl s_dz g_load g_d g_split g_tr g_pt g_arg g_e g_z g_zb g_sp g_ab
                   g_t g_l g_h g_acc g_parts s_parts g_done s_xb""".split()
        S = {n: sem(n) for n in names}
        s_adjv = [sem(f"s_adjv{k}") for k in range(OCTETS)]
        s_adjn = [sem(f"s_adjn{k}") for k in range(8)]

        block = ctx.enter_context(nc.Block())

        def gather(engine, eng, bk):
            for o, lev, live, at in LEVELS:
                if BI * bk <= at < BI * bk + BI:
                    engine.wait_ge(S["s_mx"], FIRST_ROUNDS if bk == 0 else
                                   1 + max(i for i, (n, _) in enumerate(SORT_ROUNDS) if ORDER[n // OCT] == o))
                    last = eng.tensor_copy(D[:, at:at + live, :],
                                           SRT[:, OCT * o:OCT * o + live, 2 * lev:2 * lev + 2])
            return last

        def block_views(k, first):
            shape = "p (u r) s -> p u r s"
            return (BUF[:, k, :, :].rearrange("p r (u a s) -> p a u r s", u=UB, a=PARTS),
                    D[:, first:first + BI, :].rearrange(shape, u=UB), dd[:, :, :].rearrange(shape, u=UB),
                    r1[:, :, :].rearrange(shape, u=UB), dl[:, :, :].rearrange(shape, u=UB))

        def first_parts(eng, part, dist, square, rest, rest2):
            eng.tensor_tensor(square, dist, dist, ALU.mult)
            eng.tensor_copy(part[:, 0], dist)
            return eng.tensor_tensor(part[:, 3], dist, dist, ALU.mult)

        def second_parts(eng, part, dist, square, rest, rest2):
            eng.tensor_tensor(rest, dist, part[:, 0], ALU.subtract)
            eng.tensor_tensor(part[:, 1], dist, part[:, 0], ALU.subtract)
            eng.tensor_tensor(rest2, square, part[:, 3], ALU.subtract)
            return eng.tensor_tensor(part[:, 4], square, part[:, 3], ALU.subtract)

        def third_parts(eng, part, dist, square, rest, rest2):
            eng.tensor_tensor(part[:, 2], rest, part[:, 1], ALU.subtract)
            return eng.tensor_tensor(part[:, 5], rest2, part[:, 4], ALU.subtract)

        @block.sync
        def _(sp):
            def rows(n):
                for i2 in range(2):
                    src = adj_o[:, ORDER[n], :, i2, :]
                    sp.dma_start(V[64 * i2:64 * i2 + 64, OCT * ORDER[n]:OCT * ORDER[n] + OCT, :], src)\
                        .then_inc(s_adjv[n], 16)

            rows(0)
            rows(1)
            sp.dma_start(cf[:, :], c_f).then_inc(S["s_cst"], 16)
            sp.dma_start(ce[0:KROWS, 0:UB * 128], c_e[:, 0:UB * 128]).then_inc(S["s_cst"], 16)
            sp.wait_ge(S["s_zero"], 1)
            for a in range(2):
                sp.dma_start(w1bd[64 * a:64 * a + 64, 0, 64 * a:64 * a + 64], W1[0:64, :]).then_inc(S["s_w"], 16)
                sp.dma_start(w2bd[64 * a:64 * a + 64, 64 * a:64 * a + 64], W2).then_inc(S["s_w"], 16)
                sp.dma_start(b1c[64 * a:64 * a + 64, :], b1.rearrange("(f a) -> f a", a=1)).then_inc(S["s_w"], 16)
                sp.dma_start(b2c[64 * a:64 * a + 64, :], b2.rearrange("(f a) -> f a", a=1)).then_inc(S["s_w"], 16)
            for n in range(2, OCTETS):
                rows(n)
            for g in range(8):
                sp.dma_start(LT[:, 8 * g:8 * g + 8, :], adj[8 * g:8 * g + 8, :, :].rearrange("b i j -> i b j"))\
                    .then_inc(s_adjn[g], 16)
            sp.dma_start(X[:, :, :], x.rearrange("b i c -> i b c")).then_inc(S["s_x"], 16)
            for a in range(2):
                sp.dma_start(wl[64 * a:64 * a + 64, :, 64 * a:64 * a + 64], WL.rearrange("k a c o -> (a c) k o"))\
                    .then_inc(S["s_wl"], 16)
                for c in range(1, KCH):
                    k = min(64, NRBF - 64 * c)
                    sp.dma_start(w1bd[64 * a:64 * a + k, c, 64 * a:64 * a + 64], W1[64 * c:64 * c + k, :])\
                        .then_inc(S["s_wl"], 16)
            sp.dma_start(biasr[:, :], biasL.rearrange("a b o -> (a b) o").broadcast_to([128, F]))\
                .then_inc(S["s_wl"], 16)
            sp.dma_start(ce[0:KROWS, UB * 128:], c_e[:, UB * 128:]).then_inc(S["s_wl"], 16)
            sp.wait_ge(S["s_fl"], 1)
            general = sp.value_load(flag[0:1, 0:1])
            with sp.If(general != 0):
                with sp.Fori(0, OCTETS) as o:
                    sp.wait_ge(S["g_acc"], GSTEPS * GBLK * o + 1)
                    for i2 in range(2):
                        sp.dma_start(VG[64 * i2:64 * i2 + 64, :, :], adj_o[:, o, :, i2, :])\
                            .then_inc(S["g_load"], 16)
            for n, (g, lo, hi) in enumerate(PIECES):
                sp.wait_ge(S["s_fin"], n + 1)
                graphs = slice(GR * g + lo, GR * g + hi)
                sp.dma_start(out[graphs, :, :].rearrange("b i c -> i b c"), X[:, graphs, :]).then_inc(S["s_out"], 16)
            sp.wait_ge(S["s_out"], len(PIECES) * 16)

        @block.scalar
        def _(act):
            act.preload_act_table_set("natural_log_exp_and_others")
            act.wait_ge(S["s_cst"], 32)
            act.wait_ge(S["s_w"], 8 * 16)
            nc.scalar.activation(e0, kbias, ACT.Exp).then_inc(S["s_setA"], 1)

            def setup_layer1():
                act.wait_ge(S["s_setP"], 3)
                nc.scalar.activation(t0, PM[:, 2:3], ACT.Exp, bias=b1c[:, :]).then_inc(S["s_setA"], 1)
                act.wait_ge(S["s_setA"], 2)
                nc.scalar.activation(h0, t0, ACT.Ln, bias=1.0).then_inc(S["s_setA"], 1)

            def setup_layer2():
                act.wait_ge(S["s_setP"], 4)
                act.wait_ge(S["s_setD"], 3)
                nc.scalar.activation(tq, PM[:, 3:4], ACT.Exp, bias=b2p[:, :]).then_inc(S["s_setA"], 1)
                act.wait_ge(S["s_setA"], 4)
                nc.scalar.activation(phi0, tq, ACT.Ln, bias=1.0).then_inc(S["s_setA"], 1)

            def exp_rbf(q, k):
                act.wait_ge(S["s_arg"], q + 1)
                nc.scalar.activation(e[:, k, :], Z0[:, :], ACT.Exp).then_inc(S["s_e"], 1)

            def exp_z1(q, k, first=False):
                act.wait_ge(S["s_z1"], q + 1)
                if not first:
                    act.wait_ge(S["s_h"], q)
                nc.scalar.activation(t[:, :], Z1[:, :], ACT.Exp, bias=b1c[:, :]).then_inc(S["s_t"], 1)

            def ln_z1(q, k):
                act.wait_ge(S["s_t"], q + 1)
                nc.scalar.activation(h[:, k, :], t[:, :], ACT.Ln, bias=1.0).then_inc(S["s_h"], 1)

            def exp_z2(q, k, wait=True):
                act.wait_ge(S["s_z2"], q + 1)
                if wait:
                    act.wait_ge(S["s_p"], q - 1)
                nc.scalar.activation(y[:, k, :], Z2[:, :], ACT.Exp, bias=b2p[:, :]).then_inc(S["s_y"], 1)

            for q in range(4):
                exp_rbf(q, q % 2)
                if q == 0:
                    setup_layer1()
                if q >= 1:
                    exp_z1(q - 1, (q - 1) % 2, first=q == 1)
                if q == 1:
                    setup_layer2()
                if q >= 3:
                    exp_z2(q - 3, (q - 3) % 2, wait=False)
                if q >= 1:
                    ln_z1(q - 1, (q - 1) % 2)
            exp_rbf(4, 0)
            exp_z1(3, 1)
            exp_z2(1, 1, wait=False)
            ln_z1(3, 1)
            exp_rbf(5, 1)
            exp_z1(4, 0)
            exp_z2(2, 0)
            ln_z1(4, 0)
            with act.Fori(3, UNITS // 2 - 1) as m:
                for k in range(2):
                    exp_rbf(2 * m + k, k)
                    exp_z1(2 * m + k - 1, 1 - k)
                    exp_z2(2 * m + k - 3, 1 - k)
                    ln_z1(2 * m + k - 1, 1 - k)

            def logs(o):
                act.wait_ge(S["s_p"], -(-OCTET_END[o] // OCT))
                nc.scalar.activation(LNP.rearrange("p b (t i) -> p t i b", i=2)[:, OCT * o:OCT * o + OCT],
                                     PR[:, OCT * o:OCT * o + OCT, :].rearrange("p t (i b) -> p t i b", i=2),
                                     ACT.Ln).then_inc(S["s_lnp"], 1)

            for k in range(2):
                q = UNITS - 2 + k
                exp_rbf(q, k)
                exp_z1(q - 1, 1 - k)
                exp_z2(q - 3, 1 - k)
                ln_z1(q - 1, 1 - k)
                logs(ORDER[k])
            exp_z1(UNITS - 1, 1)
            exp_z2(UNITS - 3, 1)
            ln_z1(UNITS - 1, 1)
            logs(ORDER[2])
            exp_z2(UNITS - 2, 0)
            logs(ORDER[3])
            exp_z2(UNITS - 1, 1)
            for o in ORDER[4:]:
                logs(o)

            act.wait_ge(S["s_fl"], 1)
            general = act.value_load(flag[0:1, 0:1])
            with act.If(general != 0):
                with act.Fori(0, OCTETS * GBLK * GSTEPS) as m:
                    for c in range(KCH):
                        act.wait_ge(S["g_arg"], KCH * m + c + 1)
                        nc.scalar.activation(e[:, 0, :], Z0[:, :], ACT.Exp).then_inc(S["g_e"], 1)
                    for layer in range(2):
                        act.wait_ge(S["g_ab"], 2 * m + layer + 1)
                        nc.scalar.activation(t[:, :], y[:, 0, :], ACT.Exp, scale=-1.0).then_inc(S["g_t"], 1)
                        act.wait_ge(S["g_t"], 2 * m + layer + 1)
                        nc.scalar.activation(h[:, 1, :], t[:, :], ACT.Ln, bias=1.0).then_inc(S["g_l"], 1)
                act.wait_ge(S["g_done"], 1)

            act.wait_ge(S["s_fl"], 1)

            def copy_x1t(g):
                act.wait_ge(S["s_xt"], g + 1)
                nc.scalar.activation(x1t[:, g % 2, :, :], QT, ACT.Copy).then_inc(S["s_xte"], 1)

            def copy_half(g):
                act.wait_ge(S["s_fold"], g + 1)
                if g >= 2:
                    act.wait_ge(S["s_u1"], g)
                nc.scalar.activation(half, QF[:, :, 0, :], ACT.Copy).then_inc(S["s_hf"], 1)

            def copy_b3(g):
                act.wait_ge(S["s_q3"], g + 1)
                if g >= 2:
                    act.wait_ge(S["s_b1v"], g - 1)
                nc.scalar.activation(b3s[:, g % 2, :, :], Q3, ACT.Copy).then_inc(S["s_b3c"], 1)

            def squares1(g):
                act.wait_ge(S["s_xc1"], g + 1)
                if g >= 1:
                    act.wait_ge(S["s_vs1"], g)
                nc.scalar.activation(sq1, xc1, ACT.Square).then_inc(S["s_sq1"], 1)

            def root(n, k, graphs, ready, logs_done, done):
                act.wait_ge(ready, n + 1)
                nc.scalar.activation(lnv[:, k, graphs], vs[:, k, graphs], ACT.Ln, bias=epsc[:, :], scale=1.0 / F)\
                    .then_inc(logs_done, 1)
                act.wait_ge(logs_done, n + 1)
                nc.scalar.activation(rs[:, k, graphs], lnv[:, k, graphs], ACT.Exp, scale=-0.5).then_inc(done, 1)

            def root1(g):
                root(g, 0, slice(0, GR), S["s_vs1"], S["s_lv1"], S["s_rs1"])

            def root2(n):
                root(n, 1, slice(*PIECES[n][1:]), S["s_vs2"], S["s_lv2"], S["s_rs2"])

            def copy_b2(g):
                act.wait_ge(S["s_l2"], g + 1)
                if g >= 2:
                    act.wait_ge(S["s_xb"], g - 1)
                nc.scalar.activation(b2s[:, g % 2, :, :], Q2, ACT.Copy).then_inc(S["s_b2c"], 1)

            def squares2(n):
                g, lo, hi = PIECES[n]
                act.wait_ge(S["s_xc2"], n + 1)
                if g >= 1 and lo == 0:
                    act.wait_ge(S["s_vs2"], n)
                nc.scalar.activation(sq2[:, lo:hi, :], xc2[:, lo:hi, :], ACT.Square).then_inc(S["s_sq2"], 1)

            squares1(0)
            copy_half(1)
            root1(0)
            copy_x1t(0)
            copy_b3(0)
            squares1(1)
            root1(1)
            copy_half(2)
            copy_b2(0)
            squares1(2)
            for g in range(1, GROUPS + 1):
                if g < GROUPS:
                    copy_x1t(g)
                if g == 1:
                    root1(2)
                else:
                    root2(g - 2)
                if g + 2 < GROUPS:
                    copy_half(g + 2)
                if g < GROUPS:
                    copy_b3(g)
                if g + 2 < GROUPS:
                    squares1(g + 2)
                if g < GROUPS:
                    copy_b2(g)
                if g + 2 < GROUPS:
                    root1(g + 2)
                squares2(g - 1)
            squares2(GROUPS)
            root2(GROUPS - 1)
            root2(GROUPS)

        @block.tensor
        def _(pe):
            def mm(o, w, r, start=True, stop=True):
                return nc.tensor.matmul(o, w, r, start=start, stop=stop)

            def keep_awake(n):
                for _ in range(n):
                    mm(Z2[:, 0:512], blank[:, 0:128], blank[:, :])

            def setup_bounds():
                pe.wait_ge(S["s_w"], 8 * 16)
                pe.wait_ge(S["s_setD"], 2)
                mm(PM[:, 0:1], w2bd[:, :], nl2[:, :]).then_inc(S["s_setP"], 1)
                mm(PM[:, 1:2], w1abs[:, :], onec[:, :]).then_inc(S["s_setP"], 1)

            def setup_layer1():
                pe.wait_ge(S["s_setA"], 1)
                pe.wait_ge(S["s_setD"], 4)
                mm(PM[:, 2:3], w1bd[:, 0, :], e0).then_inc(S["s_setP"], 1)

            def setup_layer2():
                pe.wait_ge(S["s_setA"], 3)
                mm(PM[:, 3:4], w2bd[:, :], h0).then_inc(S["s_setP"], 1)

            def setup_counts():
                pe.wait_ge(S["s_setD"], 5)
                mm(PM[:, 64:128], ncap[0:64, :], diag[:, :]).then_inc(S["s_setP"], 1)

            def args(q, u, k, first=False):
                if not first:
                    pe.wait_ge(S["s_e"], q)
                for c in range(2):
                    last = mm(Z0[:, 512 * c:512 * c + 512], E[0:KROWS, 0, u, :],
                              PT[0:KROWS, k, 512 * c:512 * c + 512])
                last.then_inc(S["s_arg"], 1)

            def layer1(q, u):
                pe.wait_ge(S["s_e"], q + 1)
                pe.wait_ge(S["s_t"], q)
                for c in range(2):
                    last = mm(Z1[:, 512 * c:512 * c + 512], w1bd[:, 0, :], e[:, u % 2, 512 * c:512 * c + 512])
                last.then_inc(S["s_z1"], 1)

            def layer2(q, u):
                pe.wait_ge(S["s_h"], q + 1)
                pe.wait_ge(S["s_y"], q)
                for c in range(2):
                    last = mm(Z2[:, 512 * c:512 * c + 512], w2bd[:, :], h[:, u % 2, 512 * c:512 * c + 512])
                last.then_inc(S["s_z2"], 1)

            def transpose_block(bk, k):
                pe.wait_ge(S["s_split"], bk + 1)
                for r in range(OCT):
                    last = nc.tensor.transpose(PTP[0:PROWS, 128 * r:128 * r + 128], BUF[:, k, r, :], identb[:, :])
                last.then_inc(S["s_ptt"], 1)

            def transpose_lap(n, k):
                pe.wait_ge(S["s_stage"], n + 1)
                pe.wait_ge(S["s_ltev"], n)
                for g in range(4):
                    last = nc.tensor.transpose(PM[:, 128 * g:128 * g + 128], stage[:, k, g, :], ident)
                last.then_inc(S["s_ltt"], 1)

            pe.wait_ge(S["s_blank"], 1)
            pe.wait_ge(S["s_mx"], FIRST_ROUNDS - 3)
            keep_awake(9)
            pe.wait_ge(S["s_ident"], 1)
            pe.wait_ge(S["s_ones"], 1)
            transpose_block(0, 0)
            setup_bounds()
            pe.wait_ge(S["s_pt"], 1)
            args(0, 0, 0, first=True)
            setup_layer1()

            def block_body(bk, k, first=False, last=False, lap=True):
                for u in range(UB):
                    q = UB * bk + u
                    if lap and u in (3, 7):
                        transpose_lap(2 * (bk - 1) + (u == 7), int(u == 7))
                    if u == 4 and not last:
                        transpose_block(bk + 1, 1 - k)
                    if u < UB - 1:
                        args(q + 1, u + 1, k)
                    elif not last:
                        pe.wait_ge(S["s_pt"], bk + 2)
                        args(q + 1, 0, 1 - k)
                    layer1(q, u)
                    if first and u == 0:
                        setup_layer2()
                    if first and u == 2:
                        setup_counts()
                    if not (first and u < 2):
                        layer2(q - 2, u)

            block_body(0, 0, first=True, lap=False)
            pe.wait_ge(S["s_setD"], 6)
            for bk in range(1, NBLK):
                block_body(bk, bk % 2, last=bk == NBLK - 1)
            layer2(UNITS - 2, 0)
            layer2(UNITS - 1, 1)

            for n in range(5, OCTETS - 1):
                pe.wait_ge(S["s_lnp"], n)
                pe.wait_ge(S["s_y"], UNITS)
                keep_awake(4)
            pe.wait_ge(S["s_chk"], 1)
            mm(PM[0:1, 0:1], flagc[:, 7:8], onec[:, :]).then_inc(S["s_flp"], 1)

            pe.wait_ge(S["s_lnp"], OCTETS)
            pe.wait_ge(S["s_lt"], LTB)
            pe.wait_ge(S["s_wl2"], 1)
            pe.wait_ge(S["s_fl"], 1)
            general = pe.value_load(flag[0:1, 0:1])
            with pe.If(general != 0):
                with pe.Fori(0, OCTETS * GBLK) as n:
                    pe.wait_ge(S["g_split"], n + 1)
                    for r in range(OCT):
                        last = nc.tensor.transpose(PTP[0:PROWS, 128 * r:128 * r + 128], BUF[:, 0, r, :], identb[:, :])
                    last.then_inc(S["g_tr"], 1)
                    pe.wait_ge(S["g_pt"], n + 1)
                    for u in range(GSTEPS):
                        m = GSTEPS * n + u
                        pe.wait_ge(S["g_acc"], m + 1)
                        for c in range(KCH):
                            if c:
                                pe.wait_ge(S["g_e"], KCH * m + c)
                            for a in range(2):
                                last = mm(Z0[:, 512 * a:512 * a + 512], E[0:KROWS, c, u, :],
                                          PT[0:KROWS, 0, 512 * a:512 * a + 512])
                            last.then_inc(S["g_arg"], 1)
                            pe.wait_ge(S["g_e"], KCH * m + c + 1)
                            for a in range(2):
                                last = mm(Z1[:, 512 * a:512 * a + 512], w1bd[:, c, :], e[:, 0, 512 * a:512 * a + 512],
                                          start=c == 0, stop=c == KCH - 1)
                        last.then_inc(S["g_z"], 1)
                        pe.wait_ge(S["g_h"], m + 1)
                        for a in range(2):
                            last = mm(Z2[:, 512 * a:512 * a + 512], w2bd[:, :], h[:, 0, 512 * a:512 * a + 512])
                        last.then_inc(S["g_z"], 1)
                pe.wait_ge(S["g_done"], 1)

            def fold(g):
                if g >= 1:
                    pe.wait_ge(S["s_sf"], g)
                if g >= 2:
                    pe.wait_ge(S["s_hf"], g - 1)
                for b in range(GR):
                    last = nc.tensor.transpose(QF[:, b, :, :].rearrange("p a c -> p (a c)"), LNP[:, GR * g + b, :],
                                               ident)
                last.then_inc(S["s_fold"], 1)

            def term(o, g, w, what, lo=0, hi=GR):
                for b in range(lo, hi, 2):
                    last = mm(o[:, b:b + 2, :], x1t[:, g % 2, b // 2, :], wl[:, w, :], stop=what is None)
                    if what is not None:
                        mm(o[:, b, :], LT[:, GR * g + b, :], what[:, b, :], start=False, stop=False)
                        last = mm(o[:, b + 1, :], LT[:, GR * g + b + 1, :], what[:, b + 1, :], start=False)
                return last

            def transpose_x1(g):
                pe.wait_ge(S["s_x1"], g + 1)
                for b in range(0, GR, 2):
                    last = nc.tensor.transpose(QT[:, b // 2, :],
                                               x1s[:, g % 2, b:b + 2, :].rearrange("p b c -> p (b c)"), ident)
                last.then_inc(S["s_xt"], 1)

            def make_b3(g):
                pe.wait_ge(S["s_xte"], g + 1)
                term(Q3, g, 3, None).then_inc(S["s_q3"], 1)

            def make_b2(g):
                pe.wait_ge(S["s_b3c"], g + 1)
                term(Q2, g, 2, b3s[:, g % 2, :, :]).then_inc(S["s_l2"], 1)

            def make_b1(g):
                pe.wait_ge(S["s_b2c"], g + 1)
                term(Q1, g, 1, b2s[:, g % 2, :, :]).then_inc(S["s_l1"], 1)

            def make_result(n):
                g, lo, hi = PIECES[n]
                pe.wait_ge(S["s_b1v"], g + 1)
                if g >= 1 and lo == 0:
                    pe.wait_ge(S["s_o"], n)
                term(QO if lo == 0 else Q3, g, 0, b1s, lo, hi).then_inc(S["s_l0"], 1)

            fold(0)
            keep_awake(10)
            fold(1)
            keep_awake(15)
            transpose_x1(0)
            make_b3(0)
            fold(2)
            make_b2(0)
            make_b1(0)
            for g in range(1, GROUPS + 1):
                if g < GROUPS:
                    transpose_x1(g)
                if g + 2 < GROUPS:
                    fold(g + 2)
                if g >= 2:
                    make_b1(g - 1)
                if g < GROUPS:
                    make_b3(g)
                make_result(g - 1)
                if g < GROUPS:
                    make_b2(g)
            make_result(GROUPS)

        @block.vector
        def _(dve):
            V_ = nc.vector
            chain = [0]

            def link(ins):
                chain[0] += 1
                ins.then_inc(S["s_ch"], 1)
                dve.wait_ge(S["s_ch"], chain[0])

            V_.memset(blank[:, :], 0.0).then_inc(S["s_blank"], 1)
            V_.memset(epsc[:, :], EPS)
            V_.memset(nl2[:, :], -LOG2)
            V_.memset(onec[:, :], 1.0).then_inc(S["s_setD"], 1)

            def sort_round(i):
                first, k = SORT_ROUNDS[i]
                if first % OCT == 0 and k == 0:
                    dve.wait_ge(s_adjv[first // OCT], 32)
                pair = [OCT * ORDER[n // OCT] + n % OCT for n in (first, first + 1)]
                if k:
                    dve.wait_ge(S["s_mx"], SORT_ROUNDS.index((first, k - 1)) + 1)
                    for a in pair:
                        mr = V_.match_replace(V[:, a, :], SRT[:, a, 8 * k - 8:8 * k], V[:, a, :], 0.0)
                    link(mr)
                for a in pair:
                    last = V_.max(SRT[:, a, 8 * k:8 * k + 8], V[:, a, :])
                last.then_inc(S["s_mx"], 1)

            for i in range(FIRST_ROUNDS):
                sort_round(i)
            link(gather(dve, V_, 0))
            views = block_views(0, 0)
            first_parts(V_, *views).then_inc(S["s_parts"], 1)
            dve.wait_ge(S["s_parts"], 1)
            second_parts(V_, *views).then_inc(S["s_parts"], 1)
            dve.wait_ge(S["s_cst"], 32)
            V_.tensor_copy(identb[:, :], ident).then_inc(S["s_ident"], 1)
            dve.wait_ge(S["s_parts"], 2)
            third_parts(V_, *views).then_inc(S["s_split"], 1)
            V_.tensor_scalar(ident2[:, :], ident, 2.0, None, ALU.mult).then_inc(S["s_ident"], 1)
            dve.wait_ge(S["s_w"], 8 * 16)
            V_.scalar_tensor_tensor(w1abs[:, :], w1bd[:, 0, :], -1.0, w1bd[:, 0, :], ALU.mult, ALU.max)\
                .then_inc(S["s_setD"], 1)

            def evac_block(bk):
                dve.wait_ge(S["s_ptt"], bk + 1)
                if bk >= 2:
                    dve.wait_ge(S["s_arg"], UB * (bk - 1))
                V_.tensor_copy(PT[0:PROWS, bk % 2, :], PTP[0:PROWS, :]).then_inc(S["s_pt"], 1)

            def evac_lap(n):
                dve.wait_ge(S["s_ltt"], n + 1)
                dve.wait_ge(S["s_d"], 1 + n // 8)
                V_.tensor_tensor(LT[:, 4 * n:4 * n + 4, :], PM[:, :].rearrange("p (g i) -> p g i", g=4),
                                 dinv[:, 4 * n:4 * n + 4].unsqueeze(2).broadcast_to([128, 4, 128]), ALU.mult)\
                    .then_inc(S["s_ltev"], 1)

            counts = [0]

            def after_count():
                if counts[0]:
                    dve.wait_ge(S["s_dz"], counts[0])
                counts[0] += 1

            def kept_checks():
                dve.wait_ge(S["s_gath"], 1)
                for n in range(2):
                    at = NBLK * BI // 2 * n
                    after_count()
                    V_.tensor_scalar(junk[:, 0:NBLK * BI],
                                     D[:, at:at + NBLK * BI // 2, :].rearrange("p f s -> p (f s)"),
                                     0.0, 0.0, ALU.is_equal, ALU.add, accum_out=okz[:, 8 + n:9 + n])\
                        .then_inc(S["s_dz"], 1)
                after_count()
                V_.tensor_reduce(flagc[:, 0:1], D[:, :, :], AX.XY, ALU.max).then_inc(S["s_dz"], 1)

            def products_check(o):
                after_count()
                V_.tensor_scalar(junk[:, :], PR[:, OCT * o:OCT * o + OCT, :].rearrange("p t m -> p (t m)"), PMAX,
                                 0.0, ALU.is_le, ALU.add, accum_out=okc[:, o:o + 1]).then_inc(S["s_dz"], 1)

            def check_all_but_last():
                dve.wait_ge(S["s_dz"], DZ_ALL - 1)
                V_.tensor_reduce(flagc[:, 1:2], okz[:, 0:8], AX.X, ALU.add)
                V_.tensor_reduce(flagc[:, 2:3], okz[:, 8:10], AX.X, ALU.add)
                link(V_.tensor_reduce(zc[:, 2:3], okc[:, 1:OCTETS], AX.X, ALU.add))
                link(V_.tensor_tensor(flagc[:, 3:4], flagc[:, 2:3], flagc[:, 1:2], ALU.subtract))
                link(V_.tensor_tensor(flagc[:, 5:6], flagc[:, 3:4], zc[:, 2:3], ALU.subtract))
                link(V_.tensor_scalar(flagc[:, 4:5], flagc[:, 0:1], DMAX, None, ALU.is_le))
                link(V_.scalar_tensor_tensor(flagc[:, 6:7], zc[:, 1:2], ZMAX, flagc[:, 4:5], ALU.is_le, ALU.add))
                link(V_.tensor_tensor(flagc[:, 5:6], flagc[:, 5:6], flagc[:, 6:7], ALU.subtract))
                link(V_.tensor_scalar(flagc[:, 5:6], flagc[:, 5:6],
                                      float(2 + OCTETS * UC + B * N - 2 * NBLK * BI), None, ALU.add))

            evac_block(0)
            dve.wait_ge(S["s_setP"], 2)
            V_.tensor_tensor(b2p[:, :], PM[:, 0:1], b2c[:, :], ALU.add).then_inc(S["s_setD"], 1)
            link(V_.scalar_tensor_tensor(zc[:, 0:1], b1c[:, :], -1.0, b1c[:, :], ALU.mult, ALU.max))
            V_.tensor_tensor(zc[:, 1:2], PM[:, 1:2], zc[:, 0:1], ALU.add).then_inc(S["s_setD"], 1)
            for i in range(FIRST_ROUNDS, TWO_OCTETS):
                sort_round(i)
            dve.wait_ge(S["s_setA"], 5)
            V_.tensor_scalar(diag[:, :], ident[0:64, 0:64], phi0[0:64, :], None, ALU.mult).then_inc(S["s_setD"], 1)
            runs_done = 0
            for bk in range(NBLK):
                for u in range(UB):
                    q = UB * bk + u
                    if u == 2 and bk + 1 < NBLK:
                        evac_block(bk + 1)
                    if bk == 0:
                        dve.wait_ge(s_adjn[u], 16)
                        V_.tensor_reduce(deg[:, 8 * u:8 * u + 8], LT[:, 8 * u:8 * u + 8, :], AX.X, ALU.add)\
                            .then_inc(S["s_deg"], 1)
                    if bk == 1:
                        after_count()
                        V_.tensor_scalar(junk[:, :], LT[:, 8 * u:8 * u + 8, :].rearrange("p b j -> p (b j)"), 0.0,
                                         0.0, ALU.is_equal, ALU.add, accum_out=okz[:, u:u + 1]).then_inc(S["s_dz"], 1)
                    if q == 3:
                        dve.wait_ge(S["s_setP"], 5)
                        V_.tensor_scalar(C1[:, :], PM[:, 64:128], 1.0 - N * LOG2, None, ALU.add)\
                            .then_inc(S["s_setD"], 1)
                    if bk >= 1 and u in (2, 6):
                        evac_lap(2 * (bk - 1) + (u == 6))
                    if q == UNITS - 8:
                        dve.wait_ge(S["s_wl"], 8 * 16)
                        V_.tensor_scalar(wl[:, 0, :], wl[:, 0, :], 2.0, None, ALU.mult).then_inc(S["s_wl2"], 1)
                    if q == UNITS - 6:
                        kept_checks()
                    for i in range(TWO_OCTETS + 2 * q, min(TWO_OCTETS + 2 * q + 2, len(SORT_ROUNDS))):
                        sort_round(i)
                    if q == UNITS - 1:
                        check_all_but_last()
                    dve.wait_ge(S["s_y"], q + 1)
                    pieces = runs_of_unit(q)
                    for n, (r, live, tile, fresh, o) in enumerate(pieces):
                        src = y[:, q % 2, 128 * r:128 * (r + live)].rearrange("p (t m) -> p t m", m=128)
                        dst = PR[:, tile:tile + live, :]
                        if runs_done:
                            dve.wait_ge(S["s_run"], runs_done)
                        if fresh:
                            ins = V_.tensor_scalar(dst, src, 1.0, None, ALU.add)
                        else:
                            ins = V_.scalar_tensor_tensor(dst, src, 1.0, dst, ALU.add, ALU.mult)
                        ins.then_inc(S["s_run"], 1)
                        runs_done += 1
                    dve.wait_ge(S["s_run"], runs_done)
                    V_.sem_inc(S["s_p"], 1)
                    for n, o in enumerate(ORDER):
                        if OCT * q < OCTET_END[o] <= OCT * q + OCT:
                            products_check(o)

            dve.wait_ge(S["s_dz"], DZ_ALL)
            V_.tensor_tensor(flagc[:, 7:8], flagc[:, 5:6], okc[:, ORDER[-1]:ORDER[-1] + 1], ALU.subtract)\
                .then_inc(S["s_chk"], 1)
            dve.wait_ge(S["s_flp"], 1)
            V_.tensor_copy(flag[:, :], PM[0:1, 0:1]).then_inc(S["s_fl"], 1)

            dve.wait_ge(S["s_fl"], 1)
            general = dve.value_load(flag[0:1, 0:1])
            with dve.If(general != 0):
                dve.wait_ge(S["s_lnp"], OCTETS)
                V_.memset(V[:, :, :], 0.0).then_inc(S["g_acc"], 1)
                with dve.Fori(0, OCTETS) as o:
                    with dve.Fori(0, GBLK) as c:
                        n = GBLK * o + c
                        dve.wait_ge(S["g_load"], 32 * o + 32)
                        rows = VG.rearrange("p r (c u s) -> p c u r s", c=GBLK, u=UB)
                        V_.tensor_copy(D[:, 0:BI, :].rearrange("p (u r) s -> p u r s", u=UB), rows[:, c])\
                            .then_inc(S["g_d"], 1)
                        dve.wait_ge(S["g_tr"], n + 1)
                        V_.tensor_copy(PT[0:PROWS, 0, :], PTP[0:PROWS, :]).then_inc(S["g_pt"], 1)
                        with dve.Fori(0, GSTEPS) as u:
                            m = GSTEPS * n + u
                            for layer, (z, bias) in enumerate(((Z1, b1c), (Z2, b2p))):
                                dve.wait_ge(S["g_z"], 2 * m + layer + 1)
                                V_.tensor_scalar(junk[:, :], z[:, :], bias[:, :], None, ALU.add)\
                                    .then_inc(S["g_zb"], 1)
                                dve.wait_ge(S["g_zb"], 2 * m + layer + 1)
                                V_.scalar_tensor_tensor(y[:, 0, :], junk[:, :], -1.0, junk[:, :], ALU.mult, ALU.max)\
                                    .then_inc(S["g_ab"], 1)
                                dve.wait_ge(S["g_l"], 2 * m + layer + 1)
                                V_.scalar_tensor_tensor(h[:, 0, :], junk[:, :], 0.0, h[:, 1, :], ALU.max, ALU.add)\
                                    .then_inc(S["g_sp"], 1)
                                dve.wait_ge(S["g_sp"], 2 * m + layer + 1)
                                if layer == 0:
                                    dve.sem_inc(S["g_h"], 1)
                            sums = LNP.rearrange("p b (o i) -> p o i b", o=OCTETS)[:, o]
                            dve.wait_ge(S["g_acc"], m + 1)
                            V_.tensor_tensor(sums, sums, h[:, 0, :].rearrange("p (i b) -> p i b", b=B), ALU.add)\
                                .then_inc(S["g_acc"], 1)
                V_.memset(C1[:, :], 1.0 - N * LOG2).then_inc(S["g_done"], 1)
                dve.wait_ge(S["g_done"], 1)

            wide = [128, GR, F]

            def centre(src, dst, k, lo=0, hi=GR):
                link(V_.tensor_reduce(sm[:, k, lo:hi], src, AX.X, ALU.add))
                return V_.scalar_tensor_tensor(dst, sm[:, k, lo:hi].unsqueeze(2).broadcast_to([128, hi - lo, F]),
                                               -1.0 / F, src, ALU.mult, ALU.add)

            def variance2(n):
                _, lo, hi = PIECES[n]
                dve.wait_ge(S["s_sq2"], n + 1)
                V_.tensor_reduce(vs[:, 1, lo:hi], sq2[:, lo:hi, :], AX.X, ALU.add).then_inc(S["s_vs2"], 1)

            def finish(n):
                g, lo, hi = PIECES[n]
                dve.wait_ge(S["s_rs2"], n + 1)
                V_.tensor_tensor(X[:, GR * g + lo:GR * g + hi, :], xc2[:, lo:hi, :],
                                 rs[:, 1, lo:hi].unsqueeze(2).broadcast_to([128, hi - lo, F]), ALU.mult)\
                    .then_inc(S["s_fin"], 1)

            def start2(n):
                g, lo, hi = PIECES[n]
                dve.wait_ge(S["s_l0"], n + 1)
                dve.wait_ge(S["s_xb"], g + 1)
                if n >= 1:
                    dve.wait_ge(S["s_xc2"], n)
                V_.scalar_tensor_tensor(v3[:, lo:hi, :], (QO if lo == 0 else Q3)[:, lo:hi, :], 0.5,
                                        xb[:, g % 2, lo:hi, :], ALU.mult, ALU.add).then_inc(S["s_o"], 1)
                dve.wait_ge(S["s_o"], n + 1)
                if g >= 1 and lo == 0:
                    dve.wait_ge(S["s_fin"], n)
                centre(v3[:, lo:hi, :], xc2[:, lo:hi, :], 1, lo, hi).then_inc(S["s_xc2"], 1)

            def start1(g):
                if g == 0:
                    dve.wait_ge(S["s_fold"], 1)
                    V_.tensor_tensor(v2, QF[:, :, 0, :], C1[:, :].unsqueeze(1).broadcast_to(wide), ALU.add)\
                        .then_inc(S["s_u1"], 1)
                else:
                    dve.wait_ge(S["s_xc1"], g)
                dve.wait_ge(S["s_u1"], g + 1)
                V_.tensor_tensor(v, QF[:, :, 1, :], v2, ALU.add).then_inc(S["s_sf"], 1)
                dve.wait_ge(S["s_sf"], g + 1)
                link(V_.tensor_tensor(v, v, X[:, GR * g:GR * g + GR, :], ALU.mult))
                if g >= 1:
                    dve.wait_ge(S["s_x1"], g)
                centre(v, xc1, 0).then_inc(S["s_xc1"], 1)

            dve.wait_ge(S["s_x"], 16)
            for g in range(-2, GROUPS + 2):
                if 0 <= g + 1 < GROUPS:
                    dve.wait_ge(S["s_sq1"], g + 2)
                    V_.tensor_reduce(vs[:, 0, :], sq1, AX.X, ALU.add).then_inc(S["s_vs1"], 1)
                if 0 <= g - 2 < GROUPS:
                    variance2(g - 2)
                if 0 <= g - 1 < GROUPS:
                    dve.wait_ge(S["s_l1"], g)
                    V_.tensor_tensor(b1s, Q1, b3s[:, (g - 1) % 2, :, :], ALU.subtract).then_inc(S["s_b1v"], 1)
                if 0 <= g + 1 < GROUPS:
                    dve.wait_ge(S["s_rs1"], g + 2)
                    if g + 1 >= 2:
                        dve.wait_ge(S["s_xbp"], g)
                    V_.tensor_tensor(x1s[:, (g + 1) % 2, :, :], xc1, rs[:, 0, :].unsqueeze(2).broadcast_to(wide),
                                     ALU.mult).then_inc(S["s_x1"], 1)
                if g + 2 < GROUPS:
                    start1(g + 2)
                if 0 <= g - 2 < GROUPS:
                    finish(g - 2)
                if 0 <= g - 1 < GROUPS:
                    start2(g - 1)
                if g - 1 == GROUPS - 1:
                    start2(GROUPS)
            variance2(GROUPS)
            finish(GROUPS)

        @block.gpsimd
        def _(pool):
            G = nc.gpsimd
            G.memset(w1bd[:, :, :], 0.0)
            G.memset(w2bd[:, :], 0.0)
            G.memset(wl[:, :, :], 0.0)
            G.memset(mhalf[:, :], -0.5).then_inc(S["s_zero"], 1)
            pool.wait_ge(S["s_zero"], 1)
            G.memset(PT[ONES:KROWS, :, :], 1.0).then_inc(S["s_ones"], 1)
            pool.wait_ge(S["s_ones"], 1)
            chain = [0]

            def link(ins):
                chain[0] += 1
                ins.then_inc(S["s_gch"], 1)
                pool.wait_ge(S["s_gch"], chain[0])

            def split(bk):
                if bk >= 2:
                    pool.wait_ge(S["s_ptt"], bk - 1)
                pool.wait_ge(S["s_split"], bk)
                views = block_views(bk % 2, BI * bk)
                first_parts(G, *views).then_inc(S["s_parts"], 1)
                pool.wait_ge(S["s_parts"], 2 * bk + 1)
                second_parts(G, *views).then_inc(S["s_parts"], 1)
                pool.wait_ge(S["s_parts"], 2 * bk + 2)
                third_parts(G, *views).then_inc(S["s_split"], 1)

            def scale_rows(n):
                if n >= 2:
                    pool.wait_ge(S["s_ltt"], n - 1)
                G.tensor_tensor(stage[:, n % 2, :, :], LT[:, 4 * n:4 * n + 4, :],
                                dinv2[:, 4 * n:4 * n + 4].unsqueeze(2).broadcast_to([128, 4, 128]), ALU.mult)\
                    .then_inc(S["s_stage"], 1)

            def add_diagonal(n):
                if n:
                    pool.wait_ge(S["s_lt"], n)
                link(G.tensor_tensor(ie[:, :, :], ident2[:, :].unsqueeze(1).broadcast_to([128, 4, 128]),
                                     enz[:, 4 * n:4 * n + 4].unsqueeze(2).broadcast_to([128, 4, 128]), ALU.mult))
                pool.wait_ge(S["s_ltev"], n + 1)
                G.tensor_tensor(LT[:, 4 * n:4 * n + 4, :], LT[:, 4 * n:4 * n + 4, :], ie[:, :, :], ALU.add)\
                    .then_inc(S["s_lt"], 1)

            def degree_roots(n):
                pool.wait_ge(S["s_deg"], 4 * n + 4)
                c = slice(32 * n, 32 * n + 32)
                G.tensor_scalar(enz[:, c], deg[:, c], 0.0, None, ALU.is_equal)
                G.tensor_scalar(dinv2[:, c], deg[:, c], 0.0, None, ALU.is_gt)
                link(G.tensor_scalar(dinv[:, c], deg[:, c], 1.2e-38, None, ALU.max))
                link(G.tensor_tensor(dinv[:, c], dinv[:, c], mhalf[:, c], ALU.pow))
                link(G.tensor_scalar(enz[:, c], enz[:, c], -1.0, 1.0, ALU.mult, ALU.add))
                link(G.tensor_tensor(dinv[:, c], dinv[:, c], dinv2[:, c], ALU.mult))
                G.tensor_scalar(dinv2[:, c], dinv[:, c], -2.0, None, ALU.mult).then_inc(S["s_d"], 1)
                pool.wait_ge(S["s_d"], n + 1)

            link(gather(pool, G, 1))
            split(1)
            pool.wait_ge(S["s_ident"], 2)
            degree_roots(0)
            link(gather(pool, G, 2))
            split(2)
            scale_rows(0)
            scale_rows(1)
            degree_roots(1)
            for bk in range(2, NBLK + 2):
                if bk + 1 < NBLK:
                    link(gather(pool, G, bk + 1))
                    if bk + 1 == NBLK - 1:
                        G.sem_inc(S["s_gath"], 1)
                    split(bk + 1)
                if bk < NBLK:
                    scale_rows(2 * bk - 2)
                    scale_rows(2 * bk - 1)
                if 2 * bk - 3 < LTB:
                    add_diagonal(2 * bk - 4)
                    add_diagonal(2 * bk - 3)

            pool.wait_ge(S["s_fl"], 1)
            general = pool.value_load(flag[0:1, 0:1])
            with pool.If(general != 0):
                with pool.Fori(0, OCTETS * GBLK) as n:
                    pool.wait_ge(S["g_d"], n + 1)
                    views = block_views(0, 0)
                    first_parts(G, *views).then_inc(S["g_parts"], 1)
                    pool.wait_ge(S["g_parts"], 2 * n + 1)
                    second_parts(G, *views).then_inc(S["g_parts"], 1)
                    pool.wait_ge(S["g_parts"], 2 * n + 2)
                    third_parts(G, *views).then_inc(S["g_split"], 1)
                pool.wait_ge(S["g_done"], 1)

            def half_sums(g):
                pool.wait_ge(S["s_hf"], g)
                pool.wait_ge(S["s_sf"], g)
                G.tensor_tensor(v2, half, C1[:, :].unsqueeze(1).broadcast_to([128, GR, F]), ALU.add)\
                    .then_inc(S["s_u1"], 1)

            for g in range(-2, GROUPS + 2):
                k = g % 2
                if 1 <= g + 2 < GROUPS:
                    half_sums(g + 2)
                if 0 <= g - 1 < GROUPS:
                    pool.wait_ge(S["s_b2c"], g)
                    pool.wait_ge(S["s_xbp"], g)
                    G.tensor_tensor(xb[:, 1 - k, :, :], xb[:, 1 - k, :, :], b2s[:, 1 - k, :, :], ALU.subtract)\
                        .then_inc(S["s_xb"], 1)
                if 0 <= g < GROUPS:
                    pool.wait_ge(S["s_x1"], g + 1)
                    if g >= 2:
                        pool.wait_ge(S["s_o"], g - 1)
                    G.tensor_tensor(xb[:, k, :, :], x1s[:, k, :, :],
                                    biasr[:, :].unsqueeze(1).broadcast_to([128, GR, F]), ALU.add)\
                        .then_inc(S["s_xbp"], 1)


def _bf16_bits(a):
    b = np.ascontiguousarray(a, np.float32).view(np.uint32).astype(np.uint64)
    return ((b + 0x7fff + ((b >> 16) & 1)) >> 16).astype(np.uint16)


def _constants():
    ce = np.zeros((KROWS, KCH, UB, 2, 64), np.float32)
    k = np.arange(64 * KCH).reshape(KCH, 64)
    for u in range(UB):
        for s in range(2):
            for a in range(PARTS):
                ce[(u * PARTS + a) * 2 + s, :, u, s, :] = 2 * k if a < 3 else -10.0
    rest = np.broadcast_to((-0.1 * k.astype(np.float64) ** 2)[:, None, None, :], (KCH, UB, 2, 64))
    bits = _bf16_bits(ce)
    for n in range(3):
        bits[ONES + n] = _bf16_bits(rest)
        rest = rest - (bits[ONES + n].astype(np.uint32) << 16).view(np.float32)
    cf = np.zeros((128, 1 + 128 + 128), np.float32)
    cf[:, 0] = -0.1 * (np.arange(128) % 64).astype(np.float64) ** 2
    cf[:, 1:129] = np.eye(128)
    cf[:, 129:257] = N - np.repeat(np.array(CAPS), 2)
    return bits.reshape(KROWS, -1), cf


def kernel(x, adj, L0_gnn_W1, L0_gnn_b1, L0_gnn_W2, L0_gnn_b2, L1_gnn_weight, L1_gnn_bias):
    import concourse.bacc as bacc
    from concourse.bass_utils import run_bass_kernel_spmd

    nc = bacc.Bacc("TRN2", target_bir_lowering=False, num_devices=1)
    c_e, c_f = _constants()
    arrays, args = {}, []
    for name, a in (("x", x), ("adj", adj), ("W1", L0_gnn_W1), ("b1", L0_gnn_b1), ("W2", L0_gnn_W2),
                    ("b2", L0_gnn_b2), ("WL", L1_gnn_weight), ("biasL", L1_gnn_bias), ("c_e", c_e), ("c_f", c_f)):
        a = np.ascontiguousarray(a)
        arrays[f"in_{name}"] = a
        args.append(nc.dram_tensor(f"in_{name}", a.shape, mybir.dt.from_np(a.dtype), kind="ExternalInput").ap())
    out = nc.dram_tensor("out_y", (B, N, F), mybir.dt.float32, kind="ExternalOutput").ap()
    build(nc, *args, out)
    r = run_bass_kernel_spmd(nc, [arrays], core_ids=[0])
    return r.results[0]["out_y"]
```
